# Optimizing a Trainium2 kernel written in Bass

```python
import numpy as np
import jax
import jax.numpy as jnp

def _softmax(x, axis=-1):
    return jax.nn.softmax(x, axis=axis)

def _gelu(x):
    return jax.nn.gelu(x, approximate=True)

def _silu(x):
    return jax.nn.silu(x)

def _sigmoid(x):
    return jax.nn.sigmoid(x)

def _layernorm(x, axis=-1, eps=1e-05):
    m = jnp.mean(x, axis=axis, keepdims=True)
    v = jnp.var(x, axis=axis, keepdims=True)
    return (x - m) / jnp.sqrt(v + eps)

def _scatter_add(tgt, idx, src, axis=0):
    return tgt.at[idx].add(src)

def _segment_sum(src, seg, n):
    return jax.ops.segment_sum(src, seg, n)
kernel_name = 'mk_lm_tower_d1_tok_ids768_r4_ab4a9c'

def setup_inputs(seed: int=0):
    np.random.seed(seed)
    _w = jnp.asarray

    def _rec_inputs():
        import jax
        import jax.numpy as jnp
        _rk = jax.random.key(seed)
        x = jax.random.randint(jax.random.fold_in(_rk, 1), (128, 128), 0, 8000, jnp.int32)
        return x
    x = _rec_inputs()

    def _L0_tok_setup():
        import jax, jax.numpy as jnp
        import numpy as np
        VOCAB = 8000
        D_OUT = 192
        PAD_ID = 0
        key = jax.random.key(seed)
        k1, k2 = jax.random.split(key)
        input_seq = jax.random.randint(k1, (8, 1024), 0, VOCAB, dtype=jnp.int64)
        W = jax.random.normal(k2, (D_OUT, VOCAB), dtype=jnp.float32) * 0.02
        return {'input_seq': input_seq, 'W': W}
    _L0_tok_all = _L0_tok_setup()
    _L0_tok_in = {k: v for k, v in _L0_tok_all.items() if k in ('W',)}
    del _L0_tok_all

    def _L0_attn_setup():
        import jax, jax.numpy as jnp
        import numpy as np
        NUM_HEADS = 12
        key = jax.random.key(seed)
        k1, k2, k3 = jax.random.split(key, 3)
        B, S, E = (1, 1024, 192)
        x = jax.random.normal(k1, (B, S, E), dtype=jnp.float32)
        w_qkv = jax.random.normal(k2, (E, 3 * E), dtype=jnp.float32) * 0.02
        b_qkv = jnp.zeros((3 * E,), dtype=jnp.float32)
        w_out = jax.random.normal(k3, (E, E), dtype=jnp.float32) * 0.02
        b_out = jnp.zeros((E,), dtype=jnp.float32)
        return {'x': x, 'w_qkv': w_qkv, 'b_qkv': b_qkv, 'w_out': w_out, 'b_out': b_out}
    _L0_attn_all = _L0_attn_setup()
    _L0_attn_in = {k: v for k, v in _L0_attn_all.items() if k in ('w_qkv', 'b_qkv', 'w_out', 'b_out')}
    del _L0_attn_all

    def _L0_ffn_setup():
        import jax, jax.numpy as jnp
        import numpy as np
        E = 192
        H = 12
        D = E // H
        HID = 768
        NEXP = 4
        TOPK = 2
        EPS = 1e-05

        def _ln(x, g, b):
            m = jnp.mean(x, axis=-1, keepdims=True)
            v = jnp.mean(jnp.square(x - m), axis=-1, keepdims=True)
            return (x - m) * jax.lax.rsqrt(v + EPS) * g + b
        key = jax.random.key(seed)
        ks = jax.random.split(key, 10)
        s = 0.02
        return {'x': jax.random.normal(ks[0], (8, 256, E), jnp.float32), 'ln1_g': jnp.ones((E,), jnp.float32), 'ln1_b': jnp.zeros((E,), jnp.float32), 'in_w': jax.random.normal(ks[1], (3 * E, E), jnp.float32) * s, 'in_b': jnp.zeros((3 * E,), jnp.float32), 'out_w': jax.random.normal(ks[2], (E, E), jnp.float32) * s, 'out_b': jnp.zeros((E,), jnp.float32), 'mlp_w1': jax.random.normal(ks[3], (E, HID), jnp.float32) * s, 'mlp_b1': jnp.zeros((HID,), jnp.float32), 'mlp_w2': jax.random.normal(ks[4], (HID, E), jnp.float32) * s, 'mlp_b2': jnp.zeros((E,), jnp.float32), 'ln2_g': jnp.ones((E,), jnp.float32), 'ln2_b': jnp.zeros((E,), jnp.float32), 'gate_w': jax.random.normal(ks[5], (NEXP, E), jnp.float32) * s, 'gate_b': jnp.zeros((NEXP,), jnp.float32), 'exp_w1': jax.random.normal(ks[6], (NEXP, E, HID), jnp.float32) * s, 'exp_b1': jnp.zeros((NEXP, HID), jnp.float32), 'exp_w2': jax.random.normal(ks[7], (NEXP, HID, E), jnp.float32) * s, 'exp_b2': jnp.zeros((NEXP, E), jnp.float32)}
    _L0_ffn_all = _L0_ffn_setup()
    _L0_ffn_in = {k: v for k, v in _L0_ffn_all.items() if k in ('ln1_g', 'ln1_b', 'in_w', 'in_b', 'out_w', 'out_b', 'mlp_w1', 'mlp_b1', 'mlp_w2', 'mlp_b2', 'ln2_g', 'ln2_b', 'gate_w', 'gate_b', 'exp_w1', 'exp_b1', 'exp_w2', 'exp_b2')}
    del _L0_ffn_all
    return {'x': x, 'L0_tok_W': _L0_tok_in['W'], 'L0_attn_w_qkv': _L0_attn_in['w_qkv'], 'L0_attn_b_qkv': _L0_attn_in['b_qkv'], 'L0_attn_w_out': _L0_attn_in['w_out'], 'L0_attn_b_out': _L0_attn_in['b_out'], 'L0_ffn_ln1_g': _L0_ffn_in['ln1_g'], 'L0_ffn_ln1_b': _L0_ffn_in['ln1_b'], 'L0_ffn_in_w': _L0_ffn_in['in_w'], 'L0_ffn_in_b': _L0_ffn_in['in_b'], 'L0_ffn_out_w': _L0_ffn_in['out_w'], 'L0_ffn_out_b': _L0_ffn_in['out_b'], 'L0_ffn_mlp_w1': _L0_ffn_in['mlp_w1'], 'L0_ffn_mlp_b1': _L0_ffn_in['mlp_b1'], 'L0_ffn_mlp_w2': _L0_ffn_in['mlp_w2'], 'L0_ffn_mlp_b2': _L0_ffn_in['mlp_b2'], 'L0_ffn_ln2_g': _L0_ffn_in['ln2_g'], 'L0_ffn_ln2_b': _L0_ffn_in['ln2_b'], 'L0_ffn_gate_w': _L0_ffn_in['gate_w'], 'L0_ffn_gate_b': _L0_ffn_in['gate_b'], 'L0_ffn_exp_w1': _L0_ffn_in['exp_w1'], 'L0_ffn_exp_b1': _L0_ffn_in['exp_b1'], 'L0_ffn_exp_w2': _L0_ffn_in['exp_w2'], 'L0_ffn_exp_b2': _L0_ffn_in['exp_b2']}

def reference(x, L0_tok_W, L0_attn_w_qkv, L0_attn_b_qkv, L0_attn_w_out, L0_attn_b_out, L0_ffn_ln1_g, L0_ffn_ln1_b, L0_ffn_in_w, L0_ffn_in_b, L0_ffn_out_w, L0_ffn_out_b, L0_ffn_mlp_w1, L0_ffn_mlp_b1, L0_ffn_mlp_w2, L0_ffn_mlp_b2, L0_ffn_ln2_g, L0_ffn_ln2_b, L0_ffn_gate_w, L0_ffn_gate_b, L0_ffn_exp_w1, L0_ffn_exp_b1, L0_ffn_exp_w2, L0_ffn_exp_b2):
    import jax
    import jax.numpy as jnp

    def _L0_tok_ref(input_seq, W):
        import jax, jax.numpy as jnp
        import numpy as np
        VOCAB = 8000
        D_OUT = 192
        PAD_ID = 0
        WT = W.T
        emb = jnp.take(WT, input_seq, axis=0)
        pad = (input_seq == PAD_ID)[..., None]
        return jnp.where(pad, jnp.zeros((), dtype=emb.dtype), emb)

    def _L0_attn_ref(x, w_qkv, b_qkv, w_out, b_out):
        import jax, jax.numpy as jnp
        import numpy as np
        NUM_HEADS = 12
        'Single-process (world_size==1) path of the module:\n            qkv projection -> multi-head scaled-dot-product softmax attention\n            (non-causal) -> output projection. Dropout is identity in eval.\n            '
        B, S, E = x.shape
        H = NUM_HEADS
        D = E // H
        scale = 1.0 / jnp.sqrt(jnp.asarray(D, dtype=x.dtype))
        qkv = x @ w_qkv + b_qkv
        qkv = qkv.reshape(B, S, 3, H, D)
        qkv = jnp.transpose(qkv, (2, 0, 3, 1, 4))
        q, k, v = (qkv[0], qkv[1], qkv[2])
        scores = jnp.einsum('bhqd,bhkd->bhqk', q * scale, k)
        attn = jax.nn.softmax(scores, axis=-1)
        out = jnp.einsum('bhqk,bhkd->bhqd', attn, v)
        out = jnp.transpose(out, (0, 2, 1, 3)).reshape(B, S, E)
        return out @ w_out + b_out

    def _L0_ffn_ref(x, ln1_g, ln1_b, in_w, in_b, out_w, out_b, mlp_w1, mlp_b1, mlp_w2, mlp_b2, ln2_g, ln2_b, gate_w, gate_b, exp_w1, exp_b1, exp_w2, exp_b2):
        import jax, jax.numpy as jnp
        import numpy as np
        E = 192
        H = 12
        D = E // H
        HID = 768
        NEXP = 4
        TOPK = 2
        EPS = 1e-05

        def _ln(x, g, b):
            m = jnp.mean(x, axis=-1, keepdims=True)
            v = jnp.mean(jnp.square(x - m), axis=-1, keepdims=True)
            return (x - m) * jax.lax.rsqrt(v + EPS) * g + b
        B, N, _ = x.shape
        h = _ln(x, ln1_g, ln1_b)
        qkv = h @ in_w.T + in_b
        q, k, v = jnp.split(qkv, 3, axis=-1)
        q = q.reshape(B, N, H, D)
        k = k.reshape(B, N, H, D)
        v = v.reshape(B, N, H, D)
        scores = jnp.einsum('bqhd,bkhd->bhqk', q, k) / jnp.sqrt(jnp.float32(D))
        attn = jax.nn.softmax(scores, axis=-1)
        ctx = jnp.einsum('bhqk,bkhd->bqhd', attn, v).reshape(B, N, E)
        x = x + ctx @ out_w.T + out_b
        x = x + jax.nn.gelu(x @ mlp_w1 + mlp_b1, approximate=False) @ mlp_w2 + mlp_b2
        xm = _ln(x, ln2_g, ln2_b)
        logits = xm @ gate_w.T + gate_b
        topv, topi = jax.lax.top_k(logits, TOPK)
        gates = jax.nn.softmax(topv, axis=-1)
        onehot = jax.nn.one_hot(topi, NEXP, dtype=x.dtype)
        comb = jnp.einsum('bnk,bnke->bne', gates, onehot)
        moe_out = jnp.zeros_like(x)
        for e in range(NEXP):
            he = jax.nn.gelu(xm @ exp_w1[e] + exp_b1[e], approximate=False)
            oe = he @ exp_w2[e] + exp_b2[e]
            moe_out = moe_out + comb[..., e:e + 1] * oe
        return x + moe_out
    h = _L0_tok_ref(x, L0_tok_W)
    h = h + _L0_attn_ref(_layernorm(h, axis=-1), L0_attn_w_qkv, L0_attn_b_qkv, L0_attn_w_out, L0_attn_b_out)
    h = h + _L0_ffn_ref(_layernorm(h, axis=-1), L0_ffn_ln1_g, L0_ffn_ln1_b, L0_ffn_in_w, L0_ffn_in_b, L0_ffn_out_w, L0_ffn_out_b, L0_ffn_mlp_w1, L0_ffn_mlp_b1, L0_ffn_mlp_w2, L0_ffn_mlp_b2, L0_ffn_ln2_g, L0_ffn_ln2_b, L0_ffn_gate_w, L0_ffn_gate_b, L0_ffn_exp_w1, L0_ffn_exp_b1, L0_ffn_exp_w2, L0_ffn_exp_b2)
    return h

_drawn_inputs = setup_inputs


def setup_inputs(seed=0):
    import zlib

    import numpy as np

    out = dict(_drawn_inputs(seed))
    spreads = {'L0_attn_b_qkv': (0.0, 0.1),
     'L0_attn_b_out': (0.0, 0.1),
     'L0_ffn_ln1_g': (1.0, 0.6),
     'L0_ffn_ln1_b': (0.0, 0.589),
     'L0_ffn_in_b': (0.0, 0.293),
     'L0_ffn_out_b': (0.0, 0.1),
     'L0_ffn_mlp_b1': (0.0, 0.1),
     'L0_ffn_mlp_b2': (0.0, 0.1),
     'L0_ffn_ln2_g': (1.0, 0.2),
     'L0_ffn_ln2_b': (0.0, 0.1),
     'L0_ffn_gate_b': (0.0, 0.1),
     'L0_ffn_exp_b1': (0.0, 0.411),
     'L0_ffn_exp_b2': (0.0, 0.1)}
    factors = {}
    for name, (base, spread) in spreads.items():
        noise = np.random.default_rng([zlib.crc32(name.encode()), seed]).standard_normal(out[name].shape)
        drawn = base * np.exp(spread * noise) if base else spread * noise
        out[name] = jnp.asarray(drawn.astype(out[name].dtype))
    for name, factor in factors.items():
        out[name] = (out[name] * factor).astype(out[name].dtype)
    return out
```

```python
import concourse.bass as bass
from concourse import mybir
from contextlib import ExitStack

F32 = mybir.dt.float32
F32R = mybir.dt.float32r
I32 = mybir.dt.int32
ALU = mybir.AluOpType
ACT = mybir.ActivationFunctionType
AX = mybir.AxisListType

P = 128
E = 192
EB = E - P
EW = P + 2 * EB
H = 12
D = E // H
HID = 768
MH = HID // P
NEXP = 4
NB = 1 + NEXP
T = 4
N = T * P
QH = 4
UPL = T * H // QH
VW = 2 * D + 2
LAG = 3
EPS = 1e-5
SCALE = float(D) ** -0.5
UP = NB * MH
DN = NB * T


def merged_order():
    order = "F" + "AFF" * 3 + "A"
    order += "AF" * 4 + "A"
    order += "FAFAFA"
    order += "F" * 6 + "AF" * 4
    order += "AFAFAFAFFF" + "AF" * 4
    order += "AFAFFAFFAF" + "AF" * 4
    order += "F" * 6 + "AF" * 4
    n_a, n_f = order.count("A"), order.count("F")
    order += "A" * (ATT_STEPS - n_a) + "F" * (FFN_STEPS - n_f)
    assert order.count("A") == ATT_STEPS and order.count("F") == FFN_STEPS
    return order


ATT_STEPS = 2 * (4 + UPL + LAG + 2)
FFN_STEPS = 4 + NB * (MH + T)


def tower(nc, x_ids, W, qkv_w, qkv_b, out_w, out_b, ln1_g, ln1_b, mlp_w1, mlp_b1, mlp_w2, mlp_b2,
          ln2_g, ln2_b, gate_w, gate_b, exp_w1, exp_b1, exp_w2, exp_b2, out):
    n_seq = x_ids.shape[1]
    groups = n_seq // T
    ctx = ExitStack()
    with ctx:
        def sb(name, shape, dt=F32):
            return ctx.enter_context(nc.sbuf_tensor(name, shape, dt))

        per_group = {}
        names = {}

        def sem(name, count=0):
            s = ctx.enter_context(nc.semaphore(name))
            per_group[name] = count
            names[id(s)] = name
            return s

        names = {}

        def count(s, g, n):
            return g * per_group[names[id(s)]] + n

        def any_yet(s, g, n):
            return not isinstance(g, int) or count(s, g, n) > 0

        def apart(eng, g):
            if not isinstance(g, int):
                eng.sem_inc(unused, 1)

        bank = [ctx.enter_context(nc.psum_tensor(f"bank{i}", [P, 512], F32)) for i in range(8)]
        U, DB, A = bank[0:2], bank[2:4], bank[4:8]

        class Wide:
            def __init__(self, name, cols):
                self.cols = cols
                self.hi = sb(name + "_hi", [P, cols], F32R)
                self.lo = sb(name + "_lo", [P, cols], F32R)
                self.tail = sb(name + "_tail", [P, cols], F32R)

        wqkv = [Wide(f"wqkv{L}", 3 * E) for L in range(2)]
        wout = [Wide(f"wout{L}", E) for L in range(2)]
        w1 = [Wide(f"w1_{b}", HID) for b in range(NB)]
        wgate = Wide("wgate", NEXP)
        w2h = [sb(f"w2h_{b}", [P, MH, E], F32R) for b in range(NB)]
        w2l = [sb(f"w2l_{b}", [P, MH, E], F32R) for b in range(NB)]

        qkb = [sb(f"qkb{L}", [P, 4]) for L in range(2)]
        b1 = sb("b1", [P, NB, MH])
        vb = [sb(f"vb{L}", [P, E]) for L in range(2)]
        ob = [sb(f"ob{L}", [P, E]) for L in range(2)]
        mb2 = sb("mb2", [P, E])
        gb = sb("gb", [P, NEXP])
        eb2 = sb("eb2", [64, NEXP, E], F32R)
        ones = sb("ones", [64, P], F32R)
        g1c = sb("g1c", [P, 2])
        b1c = sb("b1c", [P, 2])
        g2c = sb("g2c", [P, 2])
        b2c = sb("b2c", [P, 2])
        ident = sb("ident", [P, P])
        hmask = sb("hmask", [P, QH])
        before = sb("before", [P, NEXP, NEXP])
        mhalf = sb("mhalf", [P, T])

        idx = sb("idx", [P, T], I32)
        keep = sb("keep", [P, T])
        r0 = sb("r0", [P, T, EW])
        r1 = sb("r1", [P, T, E])
        nx = sb("nx", [P, T, EW])
        xa = [sb(f"xa{i}", [P, N], F32R) for i in range(4)]
        qk = sb("qk", [P, 4, N])
        km = sb("km", [P, 2, QH, P])
        km2 = sb("km2", [EB, QH, P])
        prob = sb("prob", [P, 2, QH, P])
        pth = sb("pth", [P, QH, P], F32R)
        ptl = sb("ptl", [P, QH, P], F32R)
        vrow = sb("vrow", [P, E])
        vhl = sb("vhl", [P, T, H, VW], F32R)
        mx = sb("mx", [P, 2, QH])
        rinv = sb("rinv", [P, 2, QH])
        osum = sb("osum", [P, QH, D])
        a_bn = sb("a_bn", [P, T, 6])
        a_mv = sb("a_mv", [P, T, 2])
        a_ve = sb("a_ve", [P, T])
        a_rs = sb("a_rs", [P, T])

        xf = sb("xf", [P, T, E])
        fa = [sb(f"fa{i}", [P, N], F32R) for i in range(4)]
        gel = sb("gel", [P, 2, N])
        n3 = gel[:, :, :].rearrange("p a n -> p (a n)").rearrange("p (t w) -> p t w", t=T)
        hh = sb("hh", [P, MH, N], F32R)
        hl = sb("hl", [P, MH, N], F32R)
        f_bn = sb("f_bn", [P, T, 6])
        f_mv = sb("f_mv", [P, T, 2])
        f_ve = sb("f_ve", [P, T])
        f_rs = sb("f_rs", [P, T])
        lg = sb("lg", [P, T, NEXP])
        gt = sb("gt", [P, T, NEXP, NEXP])
        eq = sb("eq", [P, T, NEXP, NEXP])
        sel = sb("sel", [P, T, NEXP])
        lmx = sb("lmx", [P, T])
        ldx = sb("ldx", [P, T, NEXP])
        lex = sb("lex", [P, T, NEXP])
        lsm = sb("lsm", [P, T])
        lri = sb("lri", [P, T])
        comb = sb("comb", [P, T, NEXP])

        unused = sem("unused")
        small_in = sem("small_in")
        stage_in = [sem("stage_in0"), sem("stage_in1")]
        folded = sem("folded")
        scaled = sem("scaled")
        split_hi = sem("split_hi")
        split_done = sem("split_done")
        const_ready = sem("const_ready")
        const_step = sem("const_step")
        bias_step = sem("bias_step")
        ready = sem("ready")

        idx_in = sem("idx_in", 16)
        emb_in = sem("emb_in", 16 * T)
        keep_ready = sem("keep_ready", 1)
        h0_ready = sem("h0_ready", 1)
        bn_ready = sem("bn_ready", 3)
        stats_ready = sem("stats_ready", 3)
        ve_ready = sem("ve_ready", 3)
        rstd_ready = sem("rstd_ready", 3)
        x1_ready = sem("x1_ready", 1)
        nx_ready = sem("nx_ready", 2)
        nx_dup = sem("nx_dup", 2)
        r0_bias = sem("r0_bias", 2)
        att_tr = sem("att_tr", 8)
        att_hi = sem("att_hi", 8)
        att_lo = sem("att_lo", 8)
        qk_done = sem("qk_done", 8)
        qk_out = sem("qk_out", 8)
        v_done = sem("v_done", 8)
        v_row = sem("v_row", 8)
        v_hi = sem("v_hi", 8)
        v_lo = sem("v_lo", 8)
        km_ready = sem("km_ready", 4 * T)
        s_done = sem("s_done", 2 * UPL)
        max_done = sem("max_done", 2 * UPL)
        less_max = sem("less_max", 2 * UPL)
        exp_done = sem("exp_done", 2 * UPL)
        pt_done = sem("pt_done", 2 * UPL)
        pt_hi = sem("pt_hi", 2 * UPL)
        pt_lo = sem("pt_lo", 2 * UPL)
        pv_done = sem("pv_done", 2 * UPL)
        rinv_ready = sem("rinv_ready", 2 * UPL)
        osum_ready = sem("osum_ready", 2 * UPL)
        ctx_done = sem("ctx_done", 2 * UPL)
        ctx_dup = sem("ctx_dup", 2)
        op_done = sem("op_done", 8)
        res_done = sem("res_done", 8)
        r0_dup = sem("r0_dup", 1)

        handoff = sem("handoff", 1)
        f_tr = sem("f_tr", 4)
        f_hi = sem("f_hi", 4)
        f_lo = sem("f_lo", 4)
        up_done = sem("up_done", UP)
        gelu_done = sem("gelu_done", UP)
        hid_hi = sem("hid_hi", UP)
        hid_lo = sem("hid_lo", UP)
        dn_done = sem("dn_done", DN)
        dn_out = sem("dn_out", DN)
        f_bn_ready = sem("f_bn_ready", 1)
        f_stats_ready = sem("f_stats_ready", 1)
        f_ve_ready = sem("f_ve_ready", 1)
        f_rstd_ready = sem("f_rstd_ready", 1)
        n3_ready = sem("n3_ready", 1)
        n3_dup = sem("n3_dup", 1)
        acc_init = sem("acc_init", 1)
        gate_done = sem("gate_done", 1)
        lg_ready = sem("lg_ready", 1)
        GATE_STEPS = 10
        gate_step = sem("gate_step", GATE_STEPS)
        gate_exp = sem("gate_exp", 1)
        comb_ready = sem("comb_ready", 1)
        out_written = sem("out_written", 16 * T)

        block = ctx.enter_context(nc.Block())

        stage = [qk[:, 0:2, :].rearrange("p a n -> p (a n)"), qk[:, 2:4, :].rearrange("p a n -> p (a n)")]
        pieces = []

        def wide_pieces(w, src, gain=None, job=None):
            pieces.append(("head", w, src, gain, job))
            pieces.append(("tail", w, src, gain, job))

        wide_pieces(wqkv[0], qkv_w[0])
        wide_pieces(wqkv[1], qkv_w[1], g1c, "qkv")
        wide_pieces(wout[0], out_w[0])
        wide_pieces(wout[1], out_w[1])
        wide_pieces(wgate, gate_w, g2c, "gate")
        wide_pieces(w1[0], mlp_w1)
        for e in range(NEXP):
            wide_pieces(w1[1 + e], exp_w1[e], g2c, e)
        for b in range(NB):
            src = mlp_w2 if b == 0 else exp_w2[b - 1]
            for half in range(2):
                pieces.append(("rows", b, src, None, half))
        QK_COLS = [(0, P), (P, EB), (E, P), (E + P, EB)]
        folds = [i for i, p in enumerate(pieces) if p[3] is not None]
        hm = MH // 2
        n_small = 4 * 2 + 2 + 2 * 4 + 2 * 2 + 1 + 1 + 2 + 2

        @block.sync
        def _(sp):
            def small(dst, src):
                sp.dma_start(dst, src).then_inc(small_in, 16)

            sp.wait_ge(const_ready, 1)
            for L in range(2):
                for c, (c0, m) in enumerate(QK_COLS):
                    small(qkb[L][0:m, c:c + 1], qkv_b[L][c0:c0 + m].rearrange("(p a) -> p a", a=1))
            small(b1[:, 0, :], mlp_b1)
            small(b1[:, 1:NB, :].rearrange("p e m -> p (e m)"), exp_b1)
            for t, v in ((g1c, ln1_g), (b1c, ln1_b), (g2c, ln2_g), (b2c, ln2_b)):
                small(t[:, 0:1], v[0:P].rearrange("(p a) -> p a", a=1))
                tail = v[P:E].rearrange("(p a) -> p a", a=1)
                small(t[0:EB, 1:2], tail)
            for L in range(2):
                small(vb[L][:], qkv_b[L][2 * E:3 * E].partition_broadcast(P))
                small(ob[L][:], out_b[L].partition_broadcast(P))
            small(mb2[:], mlp_b2.partition_broadcast(P))
            small(gb[:], gate_b.partition_broadcast(P))
            e2 = exp_b2.rearrange("e n -> (e n)").rearrange("(a n) -> a n", a=1)
            small(r1[0:1, :, :].rearrange("p t n -> p (t n)"), e2)
            small(r1[32:33, :, :].rearrange("p t n -> p (t n)"), e2)
            for t in (g1c, g2c):
                v = ln1_g if t is g1c else ln2_g
                small(t[EB:P, 1:2], v[P:E].rearrange("(p a) -> p a", a=1))

            for i, (kind, w, src, gain, job) in enumerate(pieces):
                if i >= 2:
                    sp.wait_ge(split_done, i - 1)
                s = stage[i % 2]
                if kind == "head":
                    sp.dma_start(s[:, 0:w.cols], src[0:P, :]).then_inc(stage_in[i % 2], 16)
                elif kind == "tail":
                    sp.dma_start(s[0:EB, 0:w.cols], src[P:E, :]).then_inc(stage_in[i % 2], 16)
                    sp.dma_start(s[EB:P, 0:w.cols], src[P:E, :]).then_inc(stage_in[i % 2], 16)
                else:
                    rows = src[job * hm * P:(job + 1) * hm * P, :]
                    sp.dma_start(s[:, 0:hm * E].rearrange("p (m n) -> p m n", m=hm),
                                 rows.rearrange("(m p) n -> p m n", p=P)).then_inc(stage_in[i % 2], 16)

            def load_idx(g):
                if any_yet(emb_in, g, 0):
                    sp.wait_ge(emb_in, count(emb_in, g, 0))
                if any_yet(keep_ready, g, 0):
                    sp.wait_ge(keep_ready, count(keep_ready, g, 0))
                sp.dma_start(idx[:, :], x_ids[:, bass.ds(g * T, T)]).then_inc(idx_in, 16)

            def store(g):
                for t in range(T):
                    sp.wait_ge(dn_out, count(dn_out, g, DN - T + t + 1))
                    sp.dma_start(out[bass.ds(g * T + t, 1), :, :].rearrange("s p n -> p (s n)"),
                                 xf[:, t, :]).then_inc(out_written, 16)

            load_idx(0)
            load_idx(1)
            store(0)
            with sp.Fori(2, groups) as g:
                load_idx(g)
                store(g - 1)
            store(groups - 1)
            sp.wait_ge(out_written, 16 * T * groups)

        def count_in(i):
            return sum(32 if pieces[j][0] == "tail" else 16 for j in range(i % 2, i + 1, 2))

        def drive(eng, attention, feed_forward):
            order = merged_order()
            for _ in attention(0):
                pass

            def both(g_att, g_ffn):
                a, f = attention(g_att), feed_forward(g_ffn)
                for c in order:
                    next(a if c == "A" else f)
                for rest in (a, f):
                    assert next(rest, None) is None

            both(1, 0)
            with eng.Fori(2, groups) as g:
                both(g, g - 1)
            for _ in feed_forward(groups - 1):
                pass

        @block.gpsimd
        def _(pool):
            step = [0]

            def const(ins, wait_too=True):
                ins.then_inc(const_step, 1)
                step[0] += 1
                if wait_too:
                    pool.wait_ge(const_step, step[0])

            for t in qkb + [g1c, b1c, g2c, b2c]:
                const(pool.memset(t[:, :], 0.0), False)
            const(pool.memset(mhalf[:, :], -0.5), False)
            const(pool.memset(ident[:, :], 0.0), False)
            const(pool.memset(hmask[:, :], 1.0), False)
            const(pool.memset(before[:, :, :], 1.0), False)
            const(pool.memset(eb2[:, :, :].bitcast(F32), 0.0), False)
            const(pool.memset(vhl[:, :, :, :].rearrange("p t h w -> p (t h w)").bitcast(F32), 1.0), False)
            const(pool.memset(ones[:, :].bitcast(F32), 1.0))
            const(pool.affine_select(out=ident[:, :], in_=ident[:, :], compare_op=ALU.not_equal, fill=1.0,
                                     base=0, pattern=[[-1, P]], channel_multiplier=1))
            const(pool.affine_select(out=before[:, :, :], in_=before[:, :, :], compare_op=ALU.is_ge, fill=0.0,
                                     base=-1, pattern=[[1, NEXP], [-1, NEXP]], channel_multiplier=0))
            for half in range(2):
                v = hmask[EB * half:EB * (half + 1), :]
                const(pool.affine_select(out=v, in_=v, compare_op=ALU.is_ge, fill=0.0, base=0,
                                         pattern=[[-D, QH]], channel_multiplier=1))
                const(pool.affine_select(out=v, in_=v, compare_op=ALU.is_ge, fill=0.0, base=D - 1,
                                         pattern=[[D, QH]], channel_multiplier=-1))
            pool.memset(a_ve[:, :], 0.0).then_inc(const_ready, 1)

            def rstd(g, stats, mv, ve, ve_sem, rs, rs_sem, n, last_use, last_n):
                if any_yet(stats, g, n):
                    pool.wait_ge(stats, count(stats, g, n))
                apart(pool, g)
                pool.tensor_scalar(ve[:, :], mv[:, :, 1], EPS, None, ALU.add).then_inc(ve_sem, 1)
                if any_yet(ve_sem, g, n):
                    pool.wait_ge(ve_sem, count(ve_sem, g, n))
                if any_yet(last_use, g, last_n):
                    pool.wait_ge(last_use, count(last_use, g, last_n))
                pool.tensor_tensor(out=rs[:, :], in0=ve[:, :], in1=mhalf[:, :], op=ALU.pow).then_inc(rs_sem, 1)

            def key_mask(g, L, t, rest):
                rows = slice(0, EB if rest else P)
                pool.wait_ge(qk_out, count(qk_out, g, 4 * L + (4 if rest else 3)))
                if any_yet(s_done, g, UPL * L + (3 * t if rest else 3 * t - 4)):
                    pool.wait_ge(s_done, count(s_done, g, UPL * L + (3 * t if rest else 3 * t - 4)))
                pool.tensor_tensor(
                    out=km2[:, :, :] if rest else km[:, t % 2, :, :],
                    in0=qk[rows, 3 if rest else 2, t * P:(t + 1) * P].unsqueeze(1).to_broadcast([rows.stop, QH, P]),
                    in1=hmask[rows, :].unsqueeze(2).to_broadcast([rows.stop, QH, P]),
                    op=ALU.mult).then_inc(km_ready, 1)

            def attention(g):
                for L in range(2):
                    if L == 0:
                        pool.wait_ge(idx_in, count(idx_in, g, 16))
                        if any_yet(handoff, g, 0):
                            pool.wait_ge(handoff, count(handoff, g, 0))
                        if any_yet(f_tr, g, -2):
                            pool.wait_ge(f_tr, count(f_tr, g, -2))
                        apart(pool, g)
                        for t in range(T):
                            pool.indirect_dma_start(
                                r0[:, t, 0:E], None, W,
                                bass.IndirectOffsetOnAxis(ap=idx[:, t:t + 1], axis=0)).then_inc(emb_in, 16)
                        rstd(g, stats_ready, a_mv, a_ve, ve_ready, a_rs, rstd_ready, 1, nx_ready, 0)
                    else:
                        rstd(g, stats_ready, a_mv, a_ve, ve_ready, a_rs, rstd_ready, 2, nx_ready, 1)
                        rstd(g, stats_ready, a_mv, a_ve, ve_ready, a_rs, rstd_ready, 3, x1_ready, 1)
                    pool.wait_ge(nx_ready, count(nx_ready, g, L + 1))
                    apart(pool, g)
                    pool.tensor_copy(nx[:, :, E:EW], nx[:, :, P:E]).then_inc(nx_dup, 1)
                    pool.tensor_tensor(out=r0[:, :, 0:E], in0=r0[:, :, 0:E],
                                       in1=ob[L][:, :].unsqueeze(1).to_broadcast([P, T, E]),
                                       op=ALU.add).then_inc(r0_bias, 1)
                    yield
                    yield
                    yield
                    key_mask(g, L, 0, False)
                    key_mask(g, L, 0, True)
                    yield
                    for s in range(UPL + LAG):
                        if s < UPL - 3 and s % 3 != 1:
                            key_mask(g, L, s // 3 + 1, s % 3 == 2)
                        yield
                    pool.wait_ge(ctx_done, count(ctx_done, g, UPL * (L + 1)))
                    apart(pool, g)
                    pool.tensor_copy(nx[:, :, E:EW], nx[:, :, P:E]).then_inc(ctx_dup, 1)
                    yield
                    if L == 1:
                        pool.wait_ge(res_done, count(res_done, g, 8))
                        apart(pool, g)
                        pool.tensor_copy(r0[:, :, E:EW], r0[:, :, P:E]).then_inc(r0_dup, 1)
                    yield

            def feed_forward(g):
                pool.wait_ge(res_done, count(res_done, g, 8))
                if any_yet(out_written, g, 0):
                    pool.wait_ge(out_written, count(out_written, g, 0))
                pool.tensor_tensor(out=xf[:, :, :], in0=r0[:, :, 0:E],
                                   in1=mb2[:, :].unsqueeze(1).to_broadcast([P, T, E]), op=ALU.add).then_inc(handoff, 1)
                yield
                for b in range(NB):
                    for m in range(MH):
                        u = MH * b + m
                        pool.wait_ge(hid_hi, count(hid_hi, g, u + 1))
                        pool.tensor_tensor(out=hl[:, m, :], in0=gel[:, u % 2, :], in1=hh[:, m, :].bitcast(F32),
                                           op=ALU.subtract).then_inc(hid_lo, 1)
                        yield
                    for t in range(T):
                        yield
                    if b == 0:
                        rstd(g, f_stats_ready, f_mv, f_ve, f_ve_ready, f_rs, f_rstd_ready, 1, n3_ready, 0)
                        pool.wait_ge(n3_ready, count(n3_ready, g, 1))
                        apart(pool, g)
                        pool.tensor_copy(n3[:, :, E:EW], n3[:, :, P:E]).then_inc(n3_dup, 1)
                        pool.tensor_tensor(out=xf[:, :, :], in0=xf[:, :, :], in1=r1[:, :, :],
                                           op=ALU.add).then_inc(acc_init, 1)
                        yield
                        yield
                        yield

            drive(pool, attention, feed_forward)

        @block.scalar
        def _(act):
            def attention(g):
                for L in range(2):
                    yield
                    for i in range(2):
                        act.wait_ge(att_tr, count(att_tr, g, 4 * L + i + 1))
                        if any_yet(op_done, g, 4 * L):
                            act.wait_ge(op_done, count(op_done, g, 4 * L))
                        act.activation(xa[2 * i][:, :], A[i][:, :], ACT.Copy).then_inc(att_hi, 1)
                    yield
                    if any_yet(s_done, g, UPL * L):
                        act.wait_ge(s_done, count(s_done, g, UPL * L))
                    if any_yet(km_ready, g, 2 * T * L):
                        act.wait_ge(km_ready, count(km_ready, g, 2 * T * L))
                    for c, bk in enumerate((2, 3, 0, 1)):
                        m = QK_COLS[c][1]
                        act.wait_ge(qk_done, count(qk_done, g, 4 * L + c + 1))
                        act.activation(qk[0:m, c, :], A[bk][0:m, :], ACT.Identity,
                                       bias=qkb[L][0:m, c:c + 1]).then_inc(qk_out, 1)
                    yield
                    yield
                    for s in range(UPL + LAG):
                        if 2 <= s < UPL + 2:
                            n = UPL * L + s - 2
                            act.wait_ge(pt_done, count(pt_done, g, n + 1))
                            if any_yet(pv_done, g, n):
                                act.wait_ge(pv_done, count(pv_done, g, n))
                            act.activation(pth[:, :, :].rearrange("p h q -> p (h q)"), A[2 + s % 2][:, :],
                                           ACT.Copy).then_inc(pt_hi, 1)
                        if s < UPL:
                            act.wait_ge(less_max, count(less_max, g, UPL * L + s + 1))
                            act.activation(prob[:, s % 2, :, :], prob[:, s % 2, :, :], ACT.Exp,
                                           scale=SCALE).then_inc(exp_done, 1)
                        yield
                    for i in range(2):
                        act.wait_ge(att_tr, count(att_tr, g, 4 * L + i + 3))
                        act.wait_ge(v_done, count(v_done, g, 4 * L + 4))
                        act.activation(xa[2 * i][:, :], A[i][:, :], ACT.Copy).then_inc(att_hi, 1)
                    yield
                    yield

            def feed_forward(g):
                def high(first):
                    for i in range(2):
                        act.wait_ge(f_tr, count(f_tr, g, first + i + 1))
                        if any_yet(up_done, g, MH if first else 0):
                            act.wait_ge(up_done, count(up_done, g, MH if first else 0))
                        if any_yet(gate_done, g, 0):
                            act.wait_ge(gate_done, count(gate_done, g, 0))
                        act.activation(fa[2 * i][:, :], DB[i][:, :], ACT.Copy).then_inc(f_hi, 1)

                high(0)
                yield
                for b in range(NB):
                    for m in range(MH):
                        u = MH * b + m
                        act.wait_ge(up_done, count(up_done, g, u + 1))
                        if any_yet(hid_lo, g, u - 1):
                            act.wait_ge(hid_lo, count(hid_lo, g, u - 1))
                        act.activation(gel[:, u % 2, :], U[u % 2][:, :], ACT.Gelu,
                                       bias=b1[:, b, m:m + 1]).then_inc(gelu_done, 1)
                        if any_yet(dn_done, g, T * b):
                            act.wait_ge(dn_done, count(dn_done, g, T * b))
                        act.activation(hh[:, m, :], U[u % 2][:, :], ACT.Gelu,
                                       bias=b1[:, b, m:m + 1]).then_inc(hid_hi, 1)
                        yield
                    for t in range(T):
                        yield
                    if b == 0:
                        yield
                        high(2)
                        yield
                        act.wait_ge(gate_step, count(gate_step, g, 7))
                        if any_yet(comb_ready, g, 0):
                            act.wait_ge(comb_ready, count(comb_ready, g, 0))
                        act.activation(lex[:, :, :], ldx[:, :, :], ACT.Exp).then_inc(gate_exp, 1)
                        yield

            act.wait_ge(ready, 1)
            drive(act, attention, feed_forward)

        @block.vector
        def _(dve):
            dve.wait_ge(const_ready, 1)
            dve.wait_ge(small_in, 16 * n_small)
            bstep = [0]

            def link(ins):
                bstep[0] += 1
                ins.then_inc(bias_step, 1)
                dve.wait_ge(bias_step, bstep[0])

            for i, (kind, w, src, gain, job) in enumerate(pieces):
                s = stage[i % 2]
                dve.wait_ge(stage_in[i % 2], count_in(i))
                if gain is not None:
                    dve.wait_ge(folded, folds.index(i) + 1)
                    col = 0 if kind == "head" else 1
                    dve.tensor_scalar(s[:, 0:w.cols], s[:, 0:w.cols], gain[:, col:col + 1], None,
                                      ALU.mult).then_inc(scaled, 1)
                    dve.wait_ge(scaled, folds.index(i) + 1)
                if kind == "rows":
                    v = s[:, 0:hm * E].rearrange("p (m n) -> p m n", m=hm)
                    sl = slice(job * hm, (job + 1) * hm)
                    dve.tensor_copy(w2h[w][:, sl, :], v).then_inc(split_hi, 1)
                    dve.wait_ge(split_hi, i + 1)
                    dve.tensor_tensor(out=w2l[w][:, sl, :], in0=v, in1=w2h[w][:, sl, :].bitcast(F32),
                                      op=ALU.subtract).then_inc(split_done, 1)
                elif kind == "head":
                    dve.tensor_copy(w.hi[:, :], s[:, 0:w.cols]).then_inc(split_hi, 1)
                    dve.wait_ge(split_hi, i + 1)
                    dve.tensor_tensor(out=w.lo[:, :], in0=s[:, 0:w.cols], in1=w.hi[:, :].bitcast(F32),
                                      op=ALU.subtract).then_inc(split_done, 1)
                else:
                    dve.tensor_copy(w.tail[:, :], s[:, 0:w.cols]).then_inc(split_hi, 1)
                    dve.wait_ge(split_hi, i + 1)
                    dve.tensor_tensor(out=w.tail[EB:P, :], in0=s[EB:P, 0:w.cols], in1=w.tail[EB:P, :].bitcast(F32),
                                      op=ALU.subtract).then_inc(split_done, 1)

            for half in range(2):
                src = U[half]
                ex = src[:, 0:NEXP * MH].rearrange("p (e m) -> p e m", e=NEXP)
                link(dve.tensor_tensor(out=b1[:, 1:NB, :], in0=ex, in1=b1[:, 1:NB, :], op=ALU.add))
                for c, (c0, m) in enumerate(QK_COLS):
                    link(dve.tensor_tensor(out=qkb[1][0:m, c:c + 1], in0=src[0:m, 24 + c:25 + c],
                                           in1=qkb[1][0:m, c:c + 1], op=ALU.add))
                link(dve.tensor_tensor(out=vb[1][:, :], in0=src[:, 64:64 + E], in1=vb[1][:, :], op=ALU.add))
                link(dve.tensor_tensor(out=gb[:, :], in0=src[:, 32:32 + NEXP], in1=gb[:, :], op=ALU.add))
            e2 = r1[:, :, :].rearrange("p t n -> p (t n)")
            eo = eb2[:, :, :].rearrange("p e n -> p (e n)")
            link(dve.tensor_copy(eo[0:1, :], e2[0:1, :]))
            link(dve.tensor_copy(eo[32:33, :], e2[32:33, :]))
            link(dve.tensor_tensor(out=eo[32:33, :], in0=e2[32:33, :], in1=eo[32:33, :].bitcast(F32),
                                   op=ALU.subtract))
            dve.memset(osum[:, :, :], 0.0).then_inc(ready, 1)

            def statistics(g, src, bn, bn_sem, mv, st_sem, n):
                for t in range(T):
                    ins = dve.bn_stats(out=bn[:, t, :], in_=src[:, t, 0:E])
                ins.then_inc(bn_sem, 1)
                if any_yet(bn_sem, g, n):
                    dve.wait_ge(bn_sem, count(bn_sem, g, n))
                apart(dve, g)
                for t in range(T):
                    ins = dve.bn_aggr(out=mv[:, t, :], in_=bn[:, t, :])
                ins.then_inc(st_sem, 1)

            def normalise(g, dst, src, mv, rs, rs_sem, n, done):
                if any_yet(rs_sem, g, n):
                    dve.wait_ge(rs_sem, count(rs_sem, g, n))
                for t in range(T):
                    ins = dve.tensor_scalar(dst[:, t, 0:E], src[:, t, 0:E], mv[:, t, 0:1], rs[:, t:t + 1],
                                            ALU.subtract, ALU.mult)
                ins.then_inc(done, 1)

            def attention(g):
                for L in range(2):
                    if L == 0:
                        dve.wait_ge(idx_in, count(idx_in, g, 16))
                        dve.tensor_scalar(keep[:, :], idx[:, :], 0, None, ALU.not_equal).then_inc(keep_ready, 1)
                        dve.wait_ge(emb_in, count(emb_in, g, 16 * T))
                        dve.wait_ge(keep_ready, count(keep_ready, g, 1))
                        for t in range(T):
                            ins = dve.tensor_scalar(r0[:, t, 0:E], r0[:, t, 0:E], keep[:, t:t + 1], None, ALU.mult)
                        ins.then_inc(h0_ready, 1)
                        dve.wait_ge(h0_ready, count(h0_ready, g, 1))
                        statistics(g, r0, a_bn, bn_ready, a_mv, stats_ready, 1)
                    else:
                        dve.wait_ge(res_done, count(res_done, g, 4))
                        statistics(g, r1, a_bn, bn_ready, a_mv, stats_ready, 2)
                        normalise(g, r0, r1, a_mv, a_rs, rstd_ready, 2, x1_ready)
                        dve.wait_ge(x1_ready, count(x1_ready, g, 1))
                        statistics(g, r0, a_bn, bn_ready, a_mv, stats_ready, 3)
                    if any_yet(att_tr, g, 4 * L):
                        dve.wait_ge(att_tr, count(att_tr, g, 4 * L))
                    normalise(g, nx, r0, a_mv, a_rs, rstd_ready, 1 if L == 0 else 3, nx_ready)
                    yield
                    for i in range(2):
                        dve.wait_ge(att_hi, count(att_hi, g, 4 * L + i + 1))
                        if any_yet(op_done, g, 4 * L):
                            dve.wait_ge(op_done, count(op_done, g, 4 * L))
                        dve.tensor_tensor(out=xa[2 * i + 1][:, :], in0=A[i][:, :], in1=xa[2 * i][:, :].bitcast(F32),
                                          op=ALU.subtract).then_inc(att_lo, 1)
                    yield
                    yield
                    if any_yet(pv_done, g, UPL * L):
                        dve.wait_ge(pv_done, count(pv_done, g, UPL * L))
                    for t in range(T):
                        dve.wait_ge(v_done, count(v_done, g, 4 * L + t + 1))
                        if any_yet(v_lo, g, 4 * L + t):
                            dve.wait_ge(v_lo, count(v_lo, g, 4 * L + t))
                        row = vrow[:, :]
                        heads = row.rearrange("p (h d) -> p h d", h=H)
                        dve.tensor_tensor(out=row, in0=A[2 + t % 2][:, 0:E], in1=vb[L][:, :],
                                          op=ALU.add).then_inc(v_row, 1)
                        dve.wait_ge(v_row, count(v_row, g, 4 * L + t + 1))
                        dve.tensor_copy(vhl[:, t, :, 0:D], heads).then_inc(v_hi, 1)
                        dve.wait_ge(v_hi, count(v_hi, g, 4 * L + t + 1))
                        dve.tensor_tensor(out=vhl[:, t, :, D:2 * D], in0=heads, in1=vhl[:, t, :, 0:D].bitcast(F32),
                                          op=ALU.subtract).then_inc(v_lo, 1)
                    yield
                    for s in range(UPL + LAG):
                        if s < UPL:
                            n = UPL * L + s
                            dve.wait_ge(s_done, count(s_done, g, n + 1))
                            scores = A[s % 2][:, :].rearrange("p (h k) -> p h k", h=QH)
                            dve.tensor_reduce(mx[:, s % 2, :], scores, AX.X, ALU.max).then_inc(max_done, 1)
                            dve.wait_ge(max_done, count(max_done, g, n + 1))
                            if any_yet(pt_done, g, n - 1):
                                dve.wait_ge(pt_done, count(pt_done, g, n - 1))
                            dve.tensor_tensor(out=prob[:, s % 2, :, :], in0=scores,
                                              in1=mx[:, s % 2, :].unsqueeze(2).to_broadcast([P, QH, P]),
                                              op=ALU.subtract).then_inc(less_max, 1)
                        if 2 <= s < UPL + 2:
                            n = UPL * L + s - 2
                            dve.wait_ge(pt_hi, count(pt_hi, g, n + 1))
                            dve.tensor_tensor(out=ptl[:, :, :].rearrange("p h q -> p (h q)"),
                                              in0=A[2 + s % 2][:, :],
                                              in1=pth[:, :, :].rearrange("p h q -> p (h q)").bitcast(F32),
                                              op=ALU.subtract).then_inc(pt_lo, 1)
                        if s >= 3:
                            u = s - 3
                            n = UPL * L + u
                            t, c = divmod(u, 3)
                            dve.wait_ge(pv_done, count(pv_done, g, n + 1))
                            o = A[2 + u % 2][:, 0:QH * VW].rearrange("p (h w) -> p h w", h=QH)
                            if any_yet(ctx_done, g, n):
                                dve.wait_ge(ctx_done, count(ctx_done, g, n))
                            dve.reciprocal(rinv[:, u % 2, :], o[:, :, 2 * D]).then_inc(rinv_ready, 1)
                            dve.tensor_reduce(osum[:, :, :], o[:, :, 0:2 * D].rearrange("p h (s d) -> p h d s", s=2),
                                              AX.X, ALU.add).then_inc(osum_ready, 1)
                            dve.wait_ge(osum_ready, count(osum_ready, g, n + 1))
                            dve.wait_ge(rinv_ready, count(rinv_ready, g, n + 1))
                            dve.wait_ge(att_tr, count(att_tr, g, 4 * L + 2))
                            dve.tensor_tensor(
                                out=nx[:, t, c * QH * D:(c + 1) * QH * D].rearrange("p (h d) -> p h d", h=QH),
                                in0=osum[:, :, :], in1=rinv[:, u % 2, :].unsqueeze(2).to_broadcast([P, QH, D]),
                                op=ALU.mult).then_inc(ctx_done, 1)
                        yield
                    for i in range(2):
                        dve.wait_ge(att_hi, count(att_hi, g, 4 * L + i + 3))
                        dve.wait_ge(v_done, count(v_done, g, 4 * L + 4))
                        dve.tensor_tensor(out=xa[2 * i + 1][:, :], in0=A[i][:, :], in1=xa[2 * i][:, :].bitcast(F32),
                                          op=ALU.subtract).then_inc(att_lo, 1)
                    yield
                    dve.wait_ge(r0_bias, count(r0_bias, g, L + 1))
                    if L == 0:
                        if any_yet(acc_init, g, 0):
                            dve.wait_ge(acc_init, count(acc_init, g, 0))
                    for t in range(T):
                        dve.wait_ge(op_done, count(op_done, g, 4 * L + t + 1))
                        dst = r1 if L == 0 else r0
                        dve.tensor_tensor(out=dst[:, t, 0:E], in0=A[2 + t % 2][:, 0:E], in1=r0[:, t, 0:E],
                                          op=ALU.add).then_inc(res_done, 1)
                    yield

            def feed_forward(g):
                def low(first):
                    for i in range(2):
                        dve.wait_ge(f_hi, count(f_hi, g, first + i + 1))
                        if any_yet(up_done, g, MH if first else 0):
                            dve.wait_ge(up_done, count(up_done, g, MH if first else 0))
                        if any_yet(gate_done, g, 0):
                            dve.wait_ge(gate_done, count(gate_done, g, 0))
                        dve.tensor_tensor(out=fa[2 * i + 1][:, :], in0=DB[i][:, :], in1=fa[2 * i][:, :].bitcast(F32),
                                          op=ALU.subtract).then_inc(f_lo, 1)

                low(0)
                yield
                for b in range(NB):
                    for m in range(MH):
                        yield
                    for t in range(T):
                        d = T * b + t
                        dve.wait_ge(dn_done, count(dn_done, g, d + 1))
                        if b == 0:
                            dve.wait_ge(handoff, count(handoff, g, 1))
                            dve.tensor_tensor(out=xf[:, t, :], in0=DB[t % 2][:, 0:E], in1=xf[:, t, :],
                                              op=ALU.add).then_inc(dn_out, 1)
                        else:
                            dve.wait_ge(acc_init, count(acc_init, g, 1))
                            dve.wait_ge(comb_ready, count(comb_ready, g, 1))
                            if any_yet(dn_out, g, d + 1 - T):
                                dve.wait_ge(dn_out, count(dn_out, g, d + 1 - T))
                            dve.scalar_tensor_tensor(out=xf[:, t, :], in0=DB[t % 2][:, 0:E],
                                                     scalar=comb[:, t, b - 1:b], in1=xf[:, t, :],
                                                     op0=ALU.mult, op1=ALU.add).then_inc(dn_out, 1)
                        yield
                    if b == 0:
                        dve.wait_ge(dn_out, count(dn_out, g, T))
                        statistics(g, xf, f_bn, f_bn_ready, f_mv, f_stats_ready, 1)
                        if any_yet(f_tr, g, 0):
                            dve.wait_ge(f_tr, count(f_tr, g, 0))
                        normalise(g, n3, xf, f_mv, f_rs, f_rstd_ready, 1, n3_ready)
                        yield
                        low(2)
                        yield
                        gate(g)
                        yield

            def gate(g):
                step = [0]

                def link(ins):
                    step[0] += 1
                    ins.then_inc(gate_step, 1)
                    dve.wait_ge(gate_step, count(gate_step, g, step[0]))

                full = [P, T, NEXP, NEXP]
                dve.wait_ge(gate_done, count(gate_done, g, 1))
                dve.tensor_tensor(out=lg[:, :, :], in0=DB[0][:, 0:T * NEXP].rearrange("p (t e) -> p t e", t=T),
                                  in1=gb[:, :].unsqueeze(1).to_broadcast([P, T, NEXP]), op=ALU.add).then_inc(lg_ready, 1)
                dve.wait_ge(lg_ready, count(lg_ready, g, 1))
                mine = lg[:, :, :].unsqueeze(3).to_broadcast(full)
                other = lg[:, :, :].unsqueeze(2).to_broadcast(full)
                link(dve.tensor_tensor(out=gt[:, :, :, :], in0=other, in1=mine, op=ALU.is_gt))
                link(dve.tensor_tensor(out=eq[:, :, :, :], in0=other, in1=mine, op=ALU.is_equal))
                link(dve.tensor_tensor(out=eq[:, :, :, :], in0=eq[:, :, :, :],
                                       in1=before[:, :, :].unsqueeze(1).to_broadcast(full), op=ALU.mult))
                link(dve.tensor_tensor(out=gt[:, :, :, :], in0=gt[:, :, :, :], in1=eq[:, :, :, :], op=ALU.add))
                link(dve.tensor_reduce(sel[:, :, :], gt[:, :, :, :], AX.X, ALU.add))
                link(dve.tensor_reduce(lmx[:, :], lg[:, :, :], AX.X, ALU.max))
                link(dve.tensor_tensor(out=ldx[:, :, :], in0=lg[:, :, :],
                                       in1=lmx[:, :].unsqueeze(2).to_broadcast([P, T, NEXP]), op=ALU.subtract))
                dve.wait_ge(gate_exp, count(gate_exp, g, 1))
                link(dve.scalar_tensor_tensor(out=sel[:, :, :], in0=sel[:, :, :], scalar=2.0, in1=lex[:, :, :],
                                              op0=ALU.is_lt, op1=ALU.mult))
                link(dve.tensor_reduce(lsm[:, :], sel[:, :, :], AX.X, ALU.add))
                link(dve.reciprocal(lri[:, :], lsm[:, :]))
                assert step[0] == GATE_STEPS
                if any_yet(dn_out, g, 0):
                    dve.wait_ge(dn_out, count(dn_out, g, 0))
                dve.tensor_tensor(out=comb[:, :, :], in0=sel[:, :, :],
                                  in1=lri[:, :].unsqueeze(2).to_broadcast([P, T, NEXP]),
                                  op=ALU.mult).then_inc(comb_ready, 1)

            drive(dve, attention, feed_forward)

        @block.tensor
        def _(pe):
            pe.wait_ge(const_ready, 1)
            pe.wait_ge(small_in, 16 * n_small)
            for i in folds:
                kind, w, src, gain, job = pieces[i]
                s = stage[i % 2]
                pe.wait_ge(stage_in[i % 2], count_in(i))
                half = 0 if kind == "head" else 1
                K = P if half == 0 else EB
                bias = (b1c if gain is g1c else b2c)[0:K, half:half + 1]
                if job == "qkv":
                    for c, (c0, m) in enumerate(QK_COLS):
                        pe.matmul(U[half][0:m, 24 + c:25 + c], s[0:K, c0:c0 + m], bias, start=True, stop=True)
                    mm = pe.matmul(U[half][:, 64:64 + E], bias.to_broadcast([K, P]), s[0:K, 2 * E:3 * E],
                                   start=True, stop=True)
                elif job == "gate":
                    mm = pe.matmul(U[half][:, 32:32 + NEXP], bias.to_broadcast([K, P]), s[0:K, 0:NEXP],
                                   start=True, stop=True)
                else:
                    for m in range(MH):
                        mm = pe.matmul(U[half][:, job * MH + m:job * MH + m + 1], s[0:K, m * P:(m + 1) * P], bias,
                                       start=True, stop=True)
                mm.then_inc(folded, 1)
            pe.wait_ge(ready, 1)

            def weights_first(dst, w, c0, m, x):
                cols = slice(c0, c0 + m)
                pe.matmul(dst, w.hi[:, cols], x[0][:, :], start=True, stop=False)
                pe.matmul(dst, w.hi[:, cols], x[1][:, :], start=False, stop=False)
                pe.matmul(dst, w.lo[:, cols], x[0][:, :], start=False, stop=False)
                pe.matmul(dst, w.tail[:, cols], x[2][:, :], start=False, stop=False)
                return pe.matmul(dst, w.tail[:, cols], x[3][:, :], start=False, stop=True)

            def tokens_first(dst, x, t, w, c0, m):
                cols, tok = slice(c0, c0 + m), slice(t * P, (t + 1) * P)
                pe.matmul(dst, x[0][:, tok], w.hi[:, cols], start=True, stop=False)
                pe.matmul(dst, x[0][:, tok], w.lo[:, cols], start=False, stop=False)
                pe.matmul(dst, x[1][:, tok], w.hi[:, cols], start=False, stop=False)
                pe.matmul(dst, x[2][:, tok], w.tail[:, cols], start=False, stop=False)
                return pe.matmul(dst, x[3][:, tok], w.tail[:, cols], start=False, stop=True)

            def to_columns(dst, src, c0):
                for t in range(T):
                    mm = pe.transpose(dst[:, t * P:(t + 1) * P], src[:, t, c0:c0 + P], ident[:, :])
                return mm

            def attention(g):
                for L in range(2):
                    yield
                    pe.wait_ge(nx_ready, count(nx_ready, g, L + 1))
                    if any_yet(att_lo, g, 4 * L - 1):
                        pe.wait_ge(att_lo, count(att_lo, g, 4 * L - 1))
                    to_columns(A[0], nx, 0).then_inc(att_tr, 1)
                    pe.wait_ge(nx_dup, count(nx_dup, g, L + 1))
                    if any_yet(att_lo, g, 4 * L):
                        pe.wait_ge(att_lo, count(att_lo, g, 4 * L))
                    to_columns(A[1], nx, P).then_inc(att_tr, 1)
                    yield
                    pe.wait_ge(att_lo, count(att_lo, g, 4 * L + 2))
                    if any_yet(res_done, g, 4 * L):
                        pe.wait_ge(res_done, count(res_done, g, 4 * L))
                    for c, bk in enumerate((2, 3, 0, 1)):
                        c0, m = QK_COLS[c]
                        weights_first(A[bk][0:m, :], wqkv[L], c0, m, xa).then_inc(qk_done, 1)
                    yield
                    for t in range(T):
                        if t < 2:
                            pe.wait_ge(qk_out, count(qk_out, g, 4 * L + t + 1))
                        else:
                            if any_yet(v_row, g, 4 * L + t - 1):
                                pe.wait_ge(v_row, count(v_row, g, 4 * L + t - 1))
                        tokens_first(A[2 + t % 2][:, 0:E], xa, t, wqkv[L], 2 * E, E).then_inc(v_done, 1)
                    yield
                    for s in range(UPL + LAG):
                        if 2 <= s < UPL + 2:
                            u = s - 2
                            n = UPL * L + u
                            pe.wait_ge(exp_done, count(exp_done, g, n + 1))
                            if u < 2:
                                pe.wait_ge(v_row, count(v_row, g, 4 * L + u + 3))
                            else:
                                pe.wait_ge(osum_ready, count(osum_ready, g, n - 1))
                            for j in range(QH):
                                mm = pe.transpose(A[2 + u % 2][:, j * P:(j + 1) * P], prob[:, u % 2, j, :], ident[:, :])
                            mm.then_inc(pt_done, 1)
                        if s < UPL:
                            n = UPL * L + s
                            t, c = divmod(s, 3)
                            rows = slice(EB * (c % 2), EB * (c % 2) + EB)
                            pe.wait_ge(qk_out, count(qk_out, g, 4 * L + 4))
                            pe.wait_ge(km_ready, count(km_ready, g, 2 * T * L + 2 * t + (2 if c == 2 else 1)))
                            if s >= 2:
                                pe.wait_ge(less_max, count(less_max, g, n - 1))
                            pe.matmul(A[s % 2][:, :], qk[rows, c // 2, t * P:(t + 1) * P],
                                      km2[:, :, :] if c == 2 else km[rows, t % 2, :, :], start=True, stop=True).then_inc(s_done, 1)
                        if s >= 3:
                            u = s - 3
                            n = UPL * L + u
                            t, c = divmod(u, 3)
                            pe.wait_ge(pt_lo, count(pt_lo, g, n + 1))
                            pe.wait_ge(v_lo, count(v_lo, g, 4 * L + t + 1))
                            for j in range(QH):
                                o = A[2 + u % 2][:, VW * j:VW * (j + 1)]
                                v = vhl[:, t, QH * c + j, :]
                                pe.matmul(o, pth[:, j, :], v, start=True, stop=False)
                                mm = pe.matmul(o, ptl[:, j, :], v, start=False, stop=True)
                            mm.then_inc(pv_done, 1)
                        yield
                    pe.wait_ge(ctx_done, count(ctx_done, g, UPL * (L + 1)))
                    pe.wait_ge(less_max, count(less_max, g, UPL * (L + 1)))
                    to_columns(A[0], nx, 0).then_inc(att_tr, 1)
                    pe.wait_ge(ctx_dup, count(ctx_dup, g, L + 1))
                    to_columns(A[1], nx, P).then_inc(att_tr, 1)
                    yield
                    pe.wait_ge(att_lo, count(att_lo, g, 4 * L + 4))
                    for t in range(T):
                        if t < 2:
                            pe.wait_ge(osum_ready, count(osum_ready, g, UPL * (L + 1) - 1 + t))
                        else:
                            if any_yet(res_done, g, 4 * L + t - 1):
                                pe.wait_ge(res_done, count(res_done, g, 4 * L + t - 1))
                        tokens_first(A[2 + t % 2][:, 0:E], xa, t, wout[L], 0, E).then_inc(op_done, 1)
                    yield

            def feed_forward(g):
                pe.wait_ge(res_done, count(res_done, g, 8))
                if any_yet(dn_out, g, 0):
                    pe.wait_ge(dn_out, count(dn_out, g, 0))
                to_columns(DB[0], r0, 0).then_inc(f_tr, 1)
                pe.wait_ge(r0_dup, count(r0_dup, g, 1))
                to_columns(DB[1], r0, P).then_inc(f_tr, 1)
                yield
                for b in range(NB):
                    for m in range(MH):
                        u = MH * b + m
                        pe.wait_ge(f_lo, count(f_lo, g, 2 if b == 0 else 4))
                        if any_yet(hid_hi, g, u - 1):
                            pe.wait_ge(hid_hi, count(hid_hi, g, u - 1))
                        weights_first(U[u % 2][:, :], w1[b], m * P, P, fa).then_inc(up_done, 1)
                        yield
                    for t in range(T):
                        d = T * b + t
                        if b == 1 and t == 0:
                            pe.wait_ge(lg_ready, count(lg_ready, g, 1))
                        elif t >= 2 or b >= 2:
                            if any_yet(dn_out, g, d - 1):
                                pe.wait_ge(dn_out, count(dn_out, g, d - 1))
                        dst, tok = DB[t % 2][:, 0:E], slice(t * P, (t + 1) * P)
                        if b > 0:
                            pe.matmul(dst, ones[:, :], eb2[:, b - 1, :], start=True, stop=False)
                        for m in range(MH):
                            if t == 0:
                                pe.wait_ge(hid_lo, count(hid_lo, g, MH * b + m + 1))
                            pe.matmul(dst, hh[:, m, tok], w2h[b][:, m, :], start=(b == 0 and m == 0), stop=False)
                            pe.matmul(dst, hh[:, m, tok], w2l[b][:, m, :], start=False, stop=False)
                            mm = pe.matmul(dst, hl[:, m, tok], w2h[b][:, m, :], start=False, stop=(m == MH - 1))
                        mm.then_inc(dn_done, 1)
                        yield
                    if b == 0:
                        yield
                        pe.wait_ge(n3_ready, count(n3_ready, g, 1))
                        pe.wait_ge(dn_out, count(dn_out, g, T))
                        to_columns(DB[0], n3, 0).then_inc(f_tr, 1)
                        pe.wait_ge(n3_dup, count(n3_dup, g, 1))
                        to_columns(DB[1], n3, P).then_inc(f_tr, 1)
                        yield
                        pe.wait_ge(f_lo, count(f_lo, g, 4))
                        for t in range(T):
                            mm = tokens_first(DB[0][:, t * NEXP:(t + 1) * NEXP], fa, t, wgate, 0, NEXP)
                        mm.then_inc(gate_done, 1)
                        yield

            drive(pe, attention, feed_forward)


def kernel(**inputs):
    import numpy as np
    import concourse.bacc as bacc
    from concourse.bass_utils import run_bass_kernel_spmd as run

    nc = bacc.Bacc("TRN2", target_bir_lowering=False, num_devices=1)
    arrays = {}

    def dram(name, a):
        a = np.ascontiguousarray(a)
        arrays[f"in_{name}"] = a
        return nc.dram_tensor(f"in_{name}", a.shape, mybir.dt.from_np(a.dtype), kind="ExternalInput").ap()

    i = {k: np.asarray(v) for k, v in inputs.items()}
    seqs, toks = i["x"].shape
    args = [
        dram("ids", i["x"].T), dram("table", i["L0_tok_W"].T),
        [dram("qkv_w0", i["L0_attn_w_qkv"]), dram("qkv_w1", i["L0_ffn_in_w"].T)],
        [dram("qkv_b0", i["L0_attn_b_qkv"]), dram("qkv_b1", i["L0_ffn_in_b"])],
        [dram("out_w0", i["L0_attn_w_out"]), dram("out_w1", i["L0_ffn_out_w"].T)],
        [dram("out_b0", i["L0_attn_b_out"]), dram("out_b1", i["L0_ffn_out_b"])],
        dram("ln1_g", i["L0_ffn_ln1_g"]), dram("ln1_b", i["L0_ffn_ln1_b"]),
        dram("mlp_w1", i["L0_ffn_mlp_w1"]), dram("mlp_b1", i["L0_ffn_mlp_b1"].reshape(MH, P).T),
        dram("mlp_w2", i["L0_ffn_mlp_w2"]), dram("mlp_b2", i["L0_ffn_mlp_b2"]),
        dram("ln2_g", i["L0_ffn_ln2_g"]), dram("ln2_b", i["L0_ffn_ln2_b"]),
        dram("gate_w", i["L0_ffn_gate_w"].T), dram("gate_b", i["L0_ffn_gate_b"]),
        dram("exp_w1", i["L0_ffn_exp_w1"]),
        dram("exp_b1", i["L0_ffn_exp_b1"].reshape(NEXP * MH, P).T),
        dram("exp_w2", i["L0_ffn_exp_w2"]), dram("exp_b2", i["L0_ffn_exp_b2"]),
    ]
    out = nc.dram_tensor("out", (seqs, toks, E), F32, kind="ExternalOutput").ap()
    tower(nc, *args, out)
    r = run(nc, [arrays], core_ids=[0])
    return r.results[0]["out"]
```

```python
import concourse.bass as bass
from concourse import mybir
from contextlib import ExitStack

F32 = mybir.dt.float32
F32R = mybir.dt.float32r
I32 = mybir.dt.int32
ALU = mybir.AluOpType
ACT = mybir.ActivationFunctionType
AX = mybir.AxisListType

P = 128
E = 192
EB = E - P
EW = P + 2 * EB
H = 12
D = E // H
HID = 768
MH = HID // P
NEXP = 4
NB = 1 + NEXP
T = 4
N = T * P
QH = 4
UPL = T * H // QH
VW = D + 1
LAG = 3
EPS = 1e-5
SCALE = float(D) ** -0.5
UP = NB * MH
DN = NB * T


def merged_order():
    order = ("AAFFFAFAFFAAAFAAFAFAFAFAFAAFAFFFFFAAFFFFAFAFAFAFFAFFFAFF"
             "AFAAFAFAFAFFAFFAFFAAFAAFAFAFFFAAFFAFFAAFAAAAAAAAAFAAFFA")
    assert order.count("A") == ATT_STEPS and order.count("F") == FFN_STEPS
    return order



ATT_STEPS = 2 * (5 + T + UPL + LAG + 3) + 1
GATE_PARTS = 3
FFN_STEPS = 3 + GATE_PARTS + NB * (MH + T)


def tower(nc, x_ids, W, qkv_w, qkv_b, out_w, out_b, ln1_g, ln1_b, mlp_w1, mlp_b1, mlp_w2, mlp_b2,
          ln2_g, ln2_b, gate_w, gate_b, exp_w1, exp_b1, exp_w2, exp_b2, out):
    n_seq = x_ids.shape[1]
    groups = n_seq // T
    ctx = ExitStack()
    with ctx:
        def sb(name, shape, dt=F32):
            return ctx.enter_context(nc.sbuf_tensor(name, shape, dt))

        per_group = {}
        names = {}

        def sem(name, count=0):
            s = ctx.enter_context(nc.semaphore(name))
            per_group[name] = count
            names[id(s)] = name
            return s

        def count(s, g, n):
            return g * per_group[names[id(s)]] + n

        def any_yet(s, g, n):
            return not isinstance(g, int) or count(s, g, n) > 0

        def apart(eng, g):
            if not isinstance(g, int):
                eng.sem_inc(unused, 1)

        bank = [ctx.enter_context(nc.psum_tensor(f"bank{i}", [P, 512], F32)) for i in range(8)]
        U, DB, OB, A = bank[0:2], bank[2], bank[3], bank[4:8]

        class Wide:
            def __init__(self, name, cols):
                self.cols = cols
                self.hi = sb(name + "_hi", [P, cols], F32R)
                self.lo = sb(name + "_lo", [P, cols], F32R)
                self.tail = sb(name + "_tail", [P, cols], F32R)

        wqkv = [Wide(f"wqkv{L}", 3 * E) for L in range(2)]
        wout = [Wide(f"wout{L}", E) for L in range(2)]
        w1 = [Wide(f"w1_{b}", HID) for b in range(NB)]
        wgate = Wide("wgate", NEXP)
        w2 = [sb(f"w2_{b}", [P, MH, E]) for b in range(NB)]

        qkb = [sb(f"qkb{L}", [P, 3]) for L in range(2)]
        b1 = sb("b1", [P, NB, MH])
        vb = [sb(f"vb{L}", [P, E]) for L in range(2)]
        ob = [sb(f"ob{L}", [P, E]) for L in range(2)]
        mb2 = sb("mb2", [P, E])
        gb = sb("gb", [P, NEXP])
        eb2 = sb("eb2", [64, NEXP, E], F32R)
        ones = sb("ones", [64, P], F32R)
        g1c = sb("g1c", [P, 2])
        b1c = sb("b1c", [P, 2])
        g2c = sb("g2c", [P, 2])
        b2c = sb("b2c", [P, 2])
        ident = sb("ident", [P, P])
        hmask = sb("hmask", [P, QH])
        before = sb("before", [P, NEXP, NEXP])
        mhalf = sb("mhalf", [P, T])

        idx = sb("idx", [P, T], I32)
        keep = sb("keep", [P, T])
        emb = sb("emb", [P, T, E])
        r0 = sb("r0", [P, T, EW])
        r1 = sb("r1", [P, T, E])
        nx = sb("nx", [P, T, EW])
        xa = [sb(f"xa{i}", [P, N], F32R) for i in range(4)]
        qk = sb("qk", [P, 4, N])
        km = sb("km", [P, 2, QH, P])
        km2 = sb("km2", [EB, QH, P])
        prob = sb("prob", [P, 2, QH, P])
        probt = sb("probt", [P, 2, QH, P])
        val = sb("val", [P, T, H, VW])
        mx = sb("mx", [P, 2, QH])
        rinv = sb("rinv", [P, 2, QH])
        a_bn = sb("a_bn", [P, T, 6])
        a_mv = sb("a_mv", [P, T, 2])
        a_ve = sb("a_ve", [P, T])
        a_rs = sb("a_rs", [P, T])

        xf = sb("xf", [P, T, E])
        fa = [sb(f"fa{i}", [P, N], F32R) for i in range(4)]
        n3 = sb("n3", [P, T, EW])
        hid = sb("hid", [P, 2, MH, N])
        f_bn = sb("f_bn", [P, T, 6])
        f_mv = sb("f_mv", [P, T, 2])
        f_ve = sb("f_ve", [P, T])
        f_rs = sb("f_rs", [P, T])
        lg = sb("lg", [P, T, NEXP])
        gt = sb("gt", [P, T, NEXP, NEXP])
        eq = sb("eq", [P, T, NEXP, NEXP])
        sel = sb("sel", [P, T, NEXP])
        lmx = sb("lmx", [P, T])
        ldx = sb("ldx", [P, T, NEXP])
        lex = sb("lex", [P, T, NEXP])
        lsm = sb("lsm", [P, T])
        lri = sb("lri", [P, T])
        comb = sb("comb", [P, T, NEXP])

        unused = sem("unused")
        small_in = sem("small_in")
        STAGES = 8
        stage_in = [sem(f"stage_in{i}") for i in range(STAGES)]
        w2_in = sem("w2_in")
        folded = sem("folded")
        scaled = sem("scaled")
        split_hi = sem("split_hi")
        split_done = sem("split_done")
        const_ready = sem("const_ready")
        const_step = sem("const_step")
        bias_step = sem("bias_step")
        ready = sem("ready")

        idx_in = sem("idx_in", 16)
        emb_in = sem("emb_in", 16 * T)
        keep_ready = sem("keep_ready", 1)
        h0_ready = sem("h0_ready", 1)
        bn_ready = sem("bn_ready", 3)
        stats_ready = sem("stats_ready", 3)
        ve_ready = sem("ve_ready", 3)
        rstd_ready = sem("rstd_ready", 3)
        x1_ready = sem("x1_ready", 1)
        nx_ready = sem("nx_ready", 2)
        r0_bias = sem("r0_bias", 2)
        att_tr = sem("att_tr", 8)
        att_hi = sem("att_hi", 8)
        att_lo = sem("att_lo", 8)
        qk_done = sem("qk_done", 6)
        qk_out = sem("qk_out", 8)
        v_done = sem("v_done", 8)
        v_out = sem("v_out", 8)
        km_ready = sem("km_ready", 4 * T)
        s_done = sem("s_done", 2 * UPL)
        max_done = sem("max_done", 2 * UPL)
        less_max = sem("less_max", 2 * UPL)
        exp_done = sem("exp_done", 2 * UPL)
        pt_done = sem("pt_done", 2 * UPL)
        pt_out = sem("pt_out", 2 * UPL)
        pv_done = sem("pv_done", 2 * UPL)
        rinv_ready = sem("rinv_ready", 2 * UPL)
        ctx_done = sem("ctx_done", 2 * UPL)
        op_done = sem("op_done", 8)
        res_done = sem("res_done", 8)
        r0_dup = sem("r0_dup", T)

        handoff = sem("handoff", 1)
        f_tr = sem("f_tr", 4)
        f_hi = sem("f_hi", 4)
        f_lo = sem("f_lo", 4)
        up_done = sem("up_done", UP)
        gelu_done = sem("gelu_done", UP)
        dn_done = sem("dn_done", DN)
        dn_out = sem("dn_out", DN)
        f_bn_ready = sem("f_bn_ready", 1)
        f_stats_ready = sem("f_stats_ready", 1)
        f_ve_ready = sem("f_ve_ready", 1)
        f_rstd_ready = sem("f_rstd_ready", 1)
        n3_ready = sem("n3_ready", 1)
        acc_init = sem("acc_init", 1)
        gate_done = sem("gate_done", 1)
        lg_ready = sem("lg_ready", 1)
        GATE_STEPS = 10
        gate_step = sem("gate_step", GATE_STEPS)
        gate_exp = sem("gate_exp", 1)
        comb_ready = sem("comb_ready", 1)
        out_written = sem("out_written", 16 * T)

        block = ctx.enter_context(nc.Block())

        hid_flat = hid[:, :, :, :].rearrange("p a m n -> p (a m n)")
        stage = [hid_flat[:, i * HID:(i + 1) * HID] for i in range(STAGES)]
        pieces = []

        def wide_pieces(w, src, gain=None, job=None):
            pieces.append(("head", w, src, gain, job))
            pieces.append(("tail", w, src, gain, job))

        wide_pieces(wqkv[0], qkv_w[0])
        wide_pieces(wout[0], out_w[0])
        wide_pieces(wout[1], out_w[1])
        wide_pieces(w1[0], mlp_w1)
        wide_pieces(wqkv[1], qkv_w[1], g1c, "qkv")
        wide_pieces(wgate, gate_w, g2c, "gate")
        for e in range(NEXP):
            wide_pieces(w1[1 + e], exp_w1[e], g2c, e)
        QK_PARTS = 3
        folds = [i for i, p in enumerate(pieces) if p[3] is not None]
        n_small = QK_PARTS * 2 + 2 + 2 * 4 + 2 * 2 + 1 + 1 + 2 + 2

        @block.sync
        def _(sp):
            def small(dst, src):
                sp.dma_start(dst, src).then_inc(small_in, 16)

            def load_piece(i):
                kind, w, src, gain, job = pieces[i]
                s = stage[i % STAGES]
                if kind == "head":
                    sp.dma_start(s[:, 0:w.cols], src[0:P, :]).then_inc(stage_in[i % STAGES], 16)
                else:
                    sp.dma_start(s[0:EB, 0:w.cols], src[P:E, :]).then_inc(stage_in[i % STAGES], 16)
                    sp.dma_start(s[EB:P, 0:w.cols], src[P:E, :]).then_inc(stage_in[i % STAGES], 16)

            for i in range(STAGES):
                load_piece(i)
            sp.wait_ge(const_ready, 1)
            for L in range(2):
                for c in range(QK_PARTS):
                    small(qkb[L][:, c:c + 1], qkv_b[L][c * P:(c + 1) * P].rearrange("(p a) -> p a", a=1))
            small(b1[:, 0, :], mlp_b1)
            small(b1[:, 1:NB, :].rearrange("p e m -> p (e m)"), exp_b1)
            for t, v in ((g1c, ln1_g), (b1c, ln1_b), (g2c, ln2_g), (b2c, ln2_b)):
                small(t[:, 0:1], v[0:P].rearrange("(p a) -> p a", a=1))
                tail = v[P:E].rearrange("(p a) -> p a", a=1)
                small(t[0:EB, 1:2], tail)
            for L in range(2):
                small(vb[L][:], qkv_b[L][2 * E:3 * E].partition_broadcast(P))
                small(ob[L][:], out_b[L].partition_broadcast(P))
            small(mb2[:], mlp_b2.partition_broadcast(P))
            small(gb[:], gate_b.partition_broadcast(P))
            e2 = exp_b2.rearrange("e n -> (e n)").rearrange("(a n) -> a n", a=1)
            small(r1[0:1, :, :].rearrange("p t n -> p (t n)"), e2)
            small(r1[32:33, :, :].rearrange("p t n -> p (t n)"), e2)
            for t in (g1c, g2c):
                v = ln1_g if t is g1c else ln2_g
                small(t[EB:P, 1:2], v[P:E].rearrange("(p a) -> p a", a=1))

            for i in range(STAGES, len(pieces)):
                sp.wait_ge(split_done, i + 1 - STAGES)
                load_piece(i)
            for b in range(NB):
                src = mlp_w2 if b == 0 else exp_w2[b - 1]
                sp.dma_start(w2[b][:, :, :], src.rearrange("(m p) n -> p m n", p=P)).then_inc(w2_in, 16)

            def load_idx(g):
                if any_yet(emb_in, g, 0):
                    sp.wait_ge(emb_in, count(emb_in, g, 0))
                if any_yet(keep_ready, g, 0):
                    sp.wait_ge(keep_ready, count(keep_ready, g, 0))
                sp.dma_start(idx[:, :], x_ids[:, bass.ds(g * T, T)]).then_inc(idx_in, 16)

            def store(g):
                for t in range(T):
                    sp.wait_ge(dn_out, count(dn_out, g, DN - T + t + 1))
                    sp.dma_start(out[bass.ds(g * T + t, 1), :, :].rearrange("s p n -> p (s n)"),
                                 xf[:, t, :]).then_inc(out_written, 16)

            load_idx(0)
            load_idx(1)
            load_idx(2)
            store(0)
            with sp.Fori(2, groups - 1) as g:
                load_idx(g + 1)
                store(g - 1)
            store(groups - 2)
            store(groups - 1)
            sp.wait_ge(out_written, 16 * T * groups)

        def count_in(i):
            return sum(32 if pieces[j][0] == "tail" else 16 for j in range(i % STAGES, i + 1, STAGES))

        def drive(eng, attention, feed_forward):
            order = merged_order()
            for _ in attention(0):
                pass

            def both(g_att, g_ffn):
                a, f = attention(g_att), feed_forward(g_ffn)
                for c in order:
                    next(a if c == "A" else f)
                for rest in (a, f):
                    assert next(rest, None) is None

            both(1, 0)
            with eng.Fori(2, groups) as g:
                both(g, g - 1)
            for _ in feed_forward(groups - 1):
                pass

        @block.gpsimd
        def _(pool):
            step = [0]

            def const(ins, wait_too=True):
                ins.then_inc(const_step, 1)
                step[0] += 1
                if wait_too:
                    pool.wait_ge(const_step, step[0])

            for t in qkb + [g1c, b1c, g2c, b2c]:
                const(pool.memset(t[:, :], 0.0), False)
            const(pool.memset(mhalf[:, :], -0.5), False)
            const(pool.memset(ident[:, :], 0.0), False)
            const(pool.memset(hmask[:, :], 1.0), False)
            const(pool.memset(before[:, :, :], 1.0), False)
            const(pool.memset(eb2[:, :, :].bitcast(F32), 0.0), False)
            const(pool.memset(val[:, :, :, :], 1.0), False)
            const(pool.memset(ones[:, :].bitcast(F32), 1.0))
            const(pool.affine_select(out=ident[:, :], in_=ident[:, :], compare_op=ALU.not_equal, fill=1.0,
                                     base=0, pattern=[[-1, P]], channel_multiplier=1))
            const(pool.affine_select(out=before[:, :, :], in_=before[:, :, :], compare_op=ALU.is_ge, fill=0.0,
                                     base=-1, pattern=[[1, NEXP], [-1, NEXP]], channel_multiplier=0))
            for half in range(2):
                v = hmask[EB * half:EB * (half + 1), :]
                const(pool.affine_select(out=v, in_=v, compare_op=ALU.is_ge, fill=0.0, base=0,
                                         pattern=[[-D, QH]], channel_multiplier=1))
                const(pool.affine_select(out=v, in_=v, compare_op=ALU.is_ge, fill=0.0, base=D - 1,
                                         pattern=[[D, QH]], channel_multiplier=-1))
            pool.memset(a_ve[:, :], 0.0).then_inc(const_ready, 1)

            def rstd(g, stats, mv, ve, ve_sem, rs, rs_sem, n, last_use, last_n):
                if any_yet(stats, g, n):
                    pool.wait_ge(stats, count(stats, g, n))
                apart(pool, g)
                pool.tensor_scalar(ve[:, :], mv[:, :, 1], EPS, None, ALU.add).then_inc(ve_sem, 1)
                if any_yet(ve_sem, g, n):
                    pool.wait_ge(ve_sem, count(ve_sem, g, n))
                if any_yet(last_use, g, last_n):
                    pool.wait_ge(last_use, count(last_use, g, last_n))
                pool.tensor_tensor(out=rs[:, :], in0=ve[:, :], in1=mhalf[:, :], op=ALU.pow).then_inc(rs_sem, 1)

            def key_mask(g, L, t, rest):
                rows = slice(0, EB if rest else P)
                pool.wait_ge(qk_out, count(qk_out, g, 4 * L + (4 if rest else 2)))
                if any_yet(s_done, g, UPL * L + (3 * t if rest else 3 * t - 4)):
                    pool.wait_ge(s_done, count(s_done, g, UPL * L + (3 * t if rest else 3 * t - 4)))
                pool.tensor_tensor(
                    out=km2[:, :, :] if rest else km[:, t % 2, :, :],
                    in0=qk[rows, 3 if rest else 2, t * P:(t + 1) * P].unsqueeze(1).to_broadcast([rows.stop, QH, P]),
                    in1=hmask[rows, :].unsqueeze(2).to_broadcast([rows.stop, QH, P]),
                    op=ALU.mult).then_inc(km_ready, 1)

            def attention(g):
                for L in range(2):
                    if L == 0:
                        pool.wait_ge(idx_in, count(idx_in, g, 16))
                        if any_yet(r0_bias, g, 0):
                            pool.wait_ge(r0_bias, count(r0_bias, g, 0))
                        apart(pool, g)
                        for t in range(T):
                            pool.indirect_dma_start(
                                emb[:, t, :], None, W,
                                bass.IndirectOffsetOnAxis(ap=idx[:, t:t + 1], axis=0)).then_inc(emb_in, 16)
                        yield
                        rstd(g, stats_ready, a_mv, a_ve, ve_ready, a_rs, rstd_ready, 1, nx_ready, 0)
                    else:
                        rstd(g, stats_ready, a_mv, a_ve, ve_ready, a_rs, rstd_ready, 2, nx_ready, 1)
                        yield
                        rstd(g, stats_ready, a_mv, a_ve, ve_ready, a_rs, rstd_ready, 3, x1_ready, 1)
                    yield
                    yield
                    yield
                    pool.wait_ge(nx_ready, count(nx_ready, g, L + 1))
                    if L == 0:
                        if any_yet(handoff, g, 0):
                            pool.wait_ge(handoff, count(handoff, g, 0))
                        if any_yet(f_tr, g, -2):
                            pool.wait_ge(f_tr, count(f_tr, g, -2))
                    pool.tensor_tensor(out=r0[:, :, 0:E], in0=(r0 if L else emb)[:, :, 0:E],
                                       in1=ob[L][:, :].unsqueeze(1).to_broadcast([P, T, E]),
                                       op=ALU.add).then_inc(r0_bias, 1)
                    yield
                    key_mask(g, L, 0, False)
                    key_mask(g, L, 0, True)
                    for t in range(T):
                        yield
                    for s in range(UPL + LAG):
                        if s < UPL - 3 and s % 3 != 1:
                            key_mask(g, L, s // 3 + 1, s % 3 == 2)
                        yield
                    yield
                    yield
                    if L == 1:
                        yield
                    yield

            def feed_forward(g):
                for b in range(NB):
                    for m in range(MH):
                        if b == 0 and m == MH // 2:
                            pool.wait_ge(res_done, count(res_done, g, 8))
                            if any_yet(out_written, g, 0):
                                pool.wait_ge(out_written, count(out_written, g, 0))
                            pool.tensor_tensor(out=xf[:, :, :], in0=r0[:, :, 0:E],
                                               in1=mb2[:, :].unsqueeze(1).to_broadcast([P, T, E]),
                                               op=ALU.add).then_inc(handoff, 1)
                        yield
                        if b == 1 and m < GATE_PARTS:
                            yield
                    for t in range(T):
                        yield
                    if b == 0:
                        rstd(g, f_stats_ready, f_mv, f_ve, f_ve_ready, f_rs, f_rstd_ready, 1, n3_ready, 0)
                        yield
                        pool.wait_ge(n3_ready, count(n3_ready, g, 1))
                        pool.tensor_tensor(out=xf[:, :, :], in0=xf[:, :, :], in1=r1[:, :, :],
                                           op=ALU.add).then_inc(acc_init, 1)
                        yield
                        yield

            drive(pool, attention, feed_forward)

        @block.scalar
        def _(act):
            def attention(g):
                for L in range(2):
                    for _ in range(3):
                        yield
                    for i in range(2):
                        act.wait_ge(att_tr, count(att_tr, g, 4 * L + i + 1))
                        if any_yet(op_done, g, 4 * L):
                            act.wait_ge(op_done, count(op_done, g, 4 * L))
                        act.activation(xa[2 * i][:, :], A[i][:, :], ACT.Copy).then_inc(att_hi, 1)
                    yield
                    if any_yet(s_done, g, UPL * L):
                        act.wait_ge(s_done, count(s_done, g, UPL * L))
                    if any_yet(km_ready, g, 2 * T * L):
                        act.wait_ge(km_ready, count(km_ready, g, 2 * T * L))
                    for c, (dst, m, part, bk, r) in enumerate(((0, P, 0, 2, 0), (2, P, 1, 3, 0),
                                                               (1, EB, 2, 0, 0), (3, EB, 2, 0, EB))):
                        act.wait_ge(qk_done, count(qk_done, g, QK_PARTS * L + part + 1))
                        act.activation(qk[0:m, dst, :], A[bk][r:r + m, :], ACT.Identity,
                                       bias=qkb[L][r:r + m, part:part + 1]).then_inc(qk_out, 1)
                    yield
                    for t in range(T):
                        yield
                    for s in range(UPL + LAG):
                        if 2 <= s < UPL + 2:
                            n = UPL * L + s - 2
                            act.wait_ge(pt_done, count(pt_done, g, n + 1))
                            if any_yet(pv_done, g, n - 1):
                                act.wait_ge(pv_done, count(pv_done, g, n - 1))
                            act.activation(probt[:, s % 2, :, :].rearrange("p h q -> p (h q)"), A[2 + s % 2][:, :],
                                           ACT.Copy).then_inc(pt_out, 1)
                        if s < UPL:
                            act.wait_ge(less_max, count(less_max, g, UPL * L + s + 1))
                            act.activation(prob[:, s % 2, :, :], prob[:, s % 2, :, :], ACT.Exp,
                                           scale=SCALE).then_inc(exp_done, 1)
                        yield
                    for i in range(2):
                        act.wait_ge(att_tr, count(att_tr, g, 4 * L + i + 3))
                        act.wait_ge(v_done, count(v_done, g, 4 * L + 4))
                        act.activation(xa[2 * i][:, :], A[i][:, :], ACT.Copy).then_inc(att_hi, 1)
                    yield
                    yield
                    yield
                high(g, 0)
                yield

            def high(g, first):
                for i in range(2):
                    act.wait_ge(f_tr, count(f_tr, g, first + i + 1))
                    if any_yet(up_done, g, MH if first else 0):
                        act.wait_ge(up_done, count(up_done, g, MH if first else 0))
                    if any_yet(gate_done, g, 0):
                        act.wait_ge(gate_done, count(gate_done, g, 0))
                    act.activation(fa[2 * i][:, :], U[i][:, :], ACT.Copy).then_inc(f_hi, 1)

            def feed_forward(g):
                for b in range(NB):
                    for m in range(MH):
                        u = MH * b + m
                        act.wait_ge(up_done, count(up_done, g, u + 1))
                        if any_yet(dn_done, g, T * max(b - 1, 0)):
                            act.wait_ge(dn_done, count(dn_done, g, T * max(b - 1, 0)))
                        act.activation(hid[:, b % 2, m, :], U[u % 2][:, :], ACT.Gelu,
                                       bias=b1[:, b, m:m + 1]).then_inc(gelu_done, 1)
                        yield
                        if b == 1 and m < GATE_PARTS:
                            if m == 1:
                                act.wait_ge(gate_step, count(gate_step, g, 7))
                                if any_yet(comb_ready, g, 0):
                                    act.wait_ge(comb_ready, count(comb_ready, g, 0))
                                act.activation(lex[:, :, :], ldx[:, :, :], ACT.Exp).then_inc(gate_exp, 1)
                            yield
                    for t in range(T):
                        yield
                    if b == 0:
                        yield
                        yield
                        high(g, 2)
                        yield

            act.wait_ge(ready, 1)
            drive(act, attention, feed_forward)

        @block.vector
        def _(dve):
            bstep = [0]

            def link(ins):
                bstep[0] += 1
                ins.then_inc(bias_step, 1)
                dve.wait_ge(bias_step, bstep[0])

            for i, (kind, w, src, gain, job) in enumerate(pieces):
                s = stage[i % STAGES]
                if i == folds[0]:
                    dve.wait_ge(const_ready, 1)
                    dve.wait_ge(small_in, 16 * n_small)
                dve.wait_ge(stage_in[i % STAGES], count_in(i))
                if gain is not None:
                    dve.wait_ge(folded, folds.index(i) + 1)
                    col = 0 if kind == "head" else 1
                    dve.tensor_scalar(s[:, 0:w.cols], s[:, 0:w.cols], gain[:, col:col + 1], None,
                                      ALU.mult).then_inc(scaled, 1)
                    dve.wait_ge(scaled, folds.index(i) + 1)
                if kind == "head":
                    dve.tensor_copy(w.hi[:, :], s[:, 0:w.cols]).then_inc(split_hi, 1)
                    dve.wait_ge(split_hi, i + 1)
                    dve.tensor_tensor(out=w.lo[:, :], in0=s[:, 0:w.cols], in1=w.hi[:, :].bitcast(F32),
                                      op=ALU.subtract).then_inc(split_done, 1)
                else:
                    dve.tensor_copy(w.tail[:, :], s[:, 0:w.cols]).then_inc(split_hi, 1)
                    dve.wait_ge(split_hi, i + 1)
                    dve.tensor_tensor(out=w.tail[EB:P, :], in0=s[EB:P, 0:w.cols], in1=w.tail[EB:P, :].bitcast(F32),
                                      op=ALU.subtract).then_inc(split_done, 1)

            for half in range(2):
                src = U[half]
                ex = src[:, 0:NEXP * MH].rearrange("p (e m) -> p e m", e=NEXP)
                link(dve.tensor_tensor(out=b1[:, 1:NB, :], in0=ex, in1=b1[:, 1:NB, :], op=ALU.add))
                link(dve.tensor_tensor(out=qkb[1][:, :], in0=src[:, 24:24 + QK_PARTS], in1=qkb[1][:, :],
                                       op=ALU.add))
                link(dve.tensor_tensor(out=vb[1][:, :], in0=src[:, 64:64 + E], in1=vb[1][:, :], op=ALU.add))
                link(dve.tensor_tensor(out=gb[:, :], in0=src[:, 32:32 + NEXP], in1=gb[:, :], op=ALU.add))
            e2 = r1[:, :, :].rearrange("p t n -> p (t n)")
            eo = eb2[:, :, :].rearrange("p e n -> p (e n)")
            link(dve.tensor_copy(eo[0:1, :], e2[0:1, :]))
            link(dve.tensor_copy(eo[32:33, :], e2[32:33, :]))
            dve.tensor_tensor(out=eo[32:33, :], in0=e2[32:33, :], in1=eo[32:33, :].bitcast(F32),
                              op=ALU.subtract).then_inc(ready, 1)

            def statistics(g, src, bn, bn_sem, mv, st_sem, n):
                for t in range(T):
                    ins = dve.bn_stats(out=bn[:, t, :], in_=src[:, t, 0:E])
                ins.then_inc(bn_sem, 1)
                if any_yet(bn_sem, g, n):
                    dve.wait_ge(bn_sem, count(bn_sem, g, n))
                apart(dve, g)
                for t in range(T):
                    ins = dve.bn_aggr(out=mv[:, t, :], in_=bn[:, t, :])
                ins.then_inc(st_sem, 1)

            def normalise(g, dst, src, mv, rs, rs_sem, n, done):
                if any_yet(rs_sem, g, n):
                    dve.wait_ge(rs_sem, count(rs_sem, g, n))
                for t in range(T):
                    for c0, c1, s0 in [(0, E, 0)] + [(E, EW, P)] * (dst is not r0):
                        ins = dve.tensor_scalar(dst[:, t, c0:c1], src[:, t, s0:E], mv[:, t, 0:1], rs[:, t:t + 1],
                                                ALU.subtract, ALU.mult)
                ins.then_inc(done, 1)

            def attention(g):
                for L in range(2):
                    if L == 0:
                        dve.wait_ge(idx_in, count(idx_in, g, 16))
                        dve.tensor_scalar(keep[:, :], idx[:, :], 0, None, ALU.not_equal).then_inc(keep_ready, 1)
                        yield
                        dve.wait_ge(emb_in, count(emb_in, g, 16 * T))
                        dve.wait_ge(keep_ready, count(keep_ready, g, 1))
                        for t in range(T):
                            ins = dve.tensor_scalar(emb[:, t, :], emb[:, t, :], keep[:, t:t + 1], None, ALU.mult)
                        ins.then_inc(h0_ready, 1)
                        dve.wait_ge(h0_ready, count(h0_ready, g, 1))
                        statistics(g, emb, a_bn, bn_ready, a_mv, stats_ready, 1)
                    else:
                        dve.wait_ge(res_done, count(res_done, g, 4))
                        statistics(g, r1, a_bn, bn_ready, a_mv, stats_ready, 2)
                        yield
                        normalise(g, r0, r1, a_mv, a_rs, rstd_ready, 2, x1_ready)
                        dve.wait_ge(x1_ready, count(x1_ready, g, 1))
                        statistics(g, r0, a_bn, bn_ready, a_mv, stats_ready, 3)
                    yield
                    if any_yet(att_tr, g, 4 * L):
                        dve.wait_ge(att_tr, count(att_tr, g, 4 * L))
                    normalise(g, nx, r0 if L else emb, a_mv, a_rs, rstd_ready, 1 if L == 0 else 3, nx_ready)
                    yield
                    for i in range(2):
                        dve.wait_ge(att_hi, count(att_hi, g, 4 * L + i + 1))
                        if any_yet(op_done, g, 4 * L):
                            dve.wait_ge(op_done, count(op_done, g, 4 * L))
                        dve.tensor_tensor(out=xa[2 * i + 1][:, :], in0=A[i][:, :], in1=xa[2 * i][:, :].bitcast(F32),
                                          op=ALU.subtract).then_inc(att_lo, 1)
                    yield
                    yield
                    if any_yet(pv_done, g, UPL * L):
                        dve.wait_ge(pv_done, count(pv_done, g, UPL * L))
                    for t in range(T):
                        dve.wait_ge(v_done, count(v_done, g, 4 * L + t + 1))
                        dve.tensor_tensor(out=val[:, t, :, 0:D],
                                          in0=A[2 + t % 2][:, 0:E].rearrange("p (h d) -> p h d", h=H),
                                          in1=vb[L][:, :].rearrange("p (h d) -> p h d", h=H),
                                          op=ALU.add).then_inc(v_out, 1)
                        yield
                    for s in range(UPL + LAG):
                        if s < UPL:
                            n = UPL * L + s
                            dve.wait_ge(s_done, count(s_done, g, n + 1))
                            scores = A[s % 2][:, :].rearrange("p (h k) -> p h k", h=QH)
                            dve.tensor_reduce(mx[:, s % 2, :], scores, AX.X, ALU.max).then_inc(max_done, 1)
                            dve.wait_ge(max_done, count(max_done, g, n + 1))
                            if any_yet(pt_done, g, n - 1):
                                dve.wait_ge(pt_done, count(pt_done, g, n - 1))
                            dve.tensor_tensor(out=prob[:, s % 2, :, :], in0=scores,
                                              in1=mx[:, s % 2, :].unsqueeze(2).to_broadcast([P, QH, P]),
                                              op=ALU.subtract).then_inc(less_max, 1)
                        if s >= 3:
                            u = s - 3
                            n = UPL * L + u
                            t, c = divmod(u, 3)
                            dve.wait_ge(pv_done, count(pv_done, g, n + 1))
                            o = OB[:, 0:QH * VW].rearrange("p (h w) -> p h w", h=QH)
                            if any_yet(ctx_done, g, n - 1):
                                dve.wait_ge(ctx_done, count(ctx_done, g, n - 1))
                            dve.reciprocal(rinv[:, u % 2, :], o[:, :, D]).then_inc(rinv_ready, 1)
                            dve.wait_ge(rinv_ready, count(rinv_ready, g, n + 1))
                            dve.wait_ge(att_tr, count(att_tr, g, 4 * L + 2))
                            for c0 in [c * QH * D] + [E] * (c == 2):
                                ins = dve.tensor_tensor(
                                    out=nx[:, t, c0:c0 + QH * D].rearrange("p (h d) -> p h d", h=QH),
                                    in0=o[:, :, 0:D], in1=rinv[:, u % 2, :].unsqueeze(2).to_broadcast([P, QH, D]),
                                    op=ALU.mult)
                            ins.then_inc(ctx_done, 1)
                        yield
                    for i in range(2):
                        dve.wait_ge(att_hi, count(att_hi, g, 4 * L + i + 3))
                        dve.wait_ge(v_done, count(v_done, g, 4 * L + 4))
                        dve.tensor_tensor(out=xa[2 * i + 1][:, :], in0=A[i][:, :], in1=xa[2 * i][:, :].bitcast(F32),
                                          op=ALU.subtract).then_inc(att_lo, 1)
                    yield
                    dve.wait_ge(r0_bias, count(r0_bias, g, L + 1))
                    if L == 0:
                        if any_yet(acc_init, g, 0):
                            dve.wait_ge(acc_init, count(acc_init, g, 0))
                    for t in range(T):
                        dve.wait_ge(op_done, count(op_done, g, 4 * L + t + 1))
                        dst = r1 if L == 0 else r0
                        if L == 1:
                            dve.tensor_tensor(out=r0[:, t, E:EW], in0=A[2 + t % 2][:, P:E], in1=r0[:, t, P:E],
                                              op=ALU.add).then_inc(r0_dup, 1)
                            dve.wait_ge(r0_dup, count(r0_dup, g, t + 1))
                        dve.tensor_tensor(out=dst[:, t, 0:E], in0=A[2 + t % 2][:, 0:E], in1=r0[:, t, 0:E],
                                          op=ALU.add).then_inc(res_done, 1)
                        if t % 2:
                            yield
                low(g, 0)
                yield

            def low(g, first):
                for i in range(2):
                    dve.wait_ge(f_hi, count(f_hi, g, first + i + 1))
                    if any_yet(up_done, g, MH if first else 0):
                        dve.wait_ge(up_done, count(up_done, g, MH if first else 0))
                    if any_yet(gate_done, g, 0):
                        dve.wait_ge(gate_done, count(gate_done, g, 0))
                    dve.tensor_tensor(out=fa[2 * i + 1][:, :], in0=U[i][:, :], in1=fa[2 * i][:, :].bitcast(F32),
                                      op=ALU.subtract).then_inc(f_lo, 1)

            def feed_forward(g):
                for b in range(NB):
                    for m in range(MH):
                        yield
                        if b == 1 and m < GATE_PARTS:
                            if m == 1:
                                gate_order(g)
                            elif m == 2:
                                gate_weights(g)
                            yield
                    for t in range(T):
                        d = T * b + t
                        dve.wait_ge(dn_done, count(dn_done, g, d + 1))
                        if b == 0:
                            dve.wait_ge(handoff, count(handoff, g, 1))
                            dve.tensor_tensor(out=xf[:, t, :], in0=DB[:, 0:E], in1=xf[:, t, :],
                                              op=ALU.add).then_inc(dn_out, 1)
                        else:
                            dve.wait_ge(acc_init, count(acc_init, g, 1))
                            dve.wait_ge(comb_ready, count(comb_ready, g, 1))
                            if any_yet(dn_out, g, d + 1 - T):
                                dve.wait_ge(dn_out, count(dn_out, g, d + 1 - T))
                            dve.scalar_tensor_tensor(out=xf[:, t, :], in0=DB[:, 0:E],
                                                     scalar=comb[:, t, b - 1:b], in1=xf[:, t, :],
                                                     op0=ALU.mult, op1=ALU.add).then_inc(dn_out, 1)
                        yield
                    if b == 0:
                        dve.wait_ge(dn_out, count(dn_out, g, T))
                        statistics(g, xf, f_bn, f_bn_ready, f_mv, f_stats_ready, 1)
                        yield
                        if any_yet(f_tr, g, 0):
                            dve.wait_ge(f_tr, count(f_tr, g, 0))
                        normalise(g, n3, xf, f_mv, f_rs, f_rstd_ready, 1, n3_ready)
                        yield
                        low(g, 2)
                        yield

            gate_steps = [0]

            def link_gate(g, ins):
                gate_steps[0] += 1
                ins.then_inc(gate_step, 1)
                dve.wait_ge(gate_step, count(gate_step, g, gate_steps[0]))

            def gate_order(g):
                gate_steps[0] = 0
                full = [P, T, NEXP, NEXP]
                dve.wait_ge(gate_done, count(gate_done, g, 1))
                dve.tensor_tensor(out=lg[:, :, :], in0=DB[:, 0:T * NEXP].rearrange("p (t e) -> p t e", t=T),
                                  in1=gb[:, :].unsqueeze(1).to_broadcast([P, T, NEXP]),
                                  op=ALU.add).then_inc(lg_ready, 1)
                dve.wait_ge(lg_ready, count(lg_ready, g, 1))
                mine = lg[:, :, :].unsqueeze(3).to_broadcast(full)
                other = lg[:, :, :].unsqueeze(2).to_broadcast(full)
                link_gate(g, dve.tensor_tensor(out=gt[:, :, :, :], in0=other, in1=mine, op=ALU.is_gt))
                link_gate(g, dve.tensor_tensor(out=eq[:, :, :, :], in0=other, in1=mine, op=ALU.is_equal))
                link_gate(g, dve.tensor_tensor(out=eq[:, :, :, :], in0=eq[:, :, :, :],
                                               in1=before[:, :, :].unsqueeze(1).to_broadcast(full), op=ALU.mult))
                link_gate(g, dve.tensor_tensor(out=gt[:, :, :, :], in0=gt[:, :, :, :], in1=eq[:, :, :, :],
                                               op=ALU.add))
                link_gate(g, dve.tensor_reduce(sel[:, :, :], gt[:, :, :, :], AX.X, ALU.add))
                link_gate(g, dve.tensor_reduce(lmx[:, :], lg[:, :, :], AX.X, ALU.max))
                link_gate(g, dve.tensor_tensor(out=ldx[:, :, :], in0=lg[:, :, :],
                                               in1=lmx[:, :].unsqueeze(2).to_broadcast([P, T, NEXP]), op=ALU.subtract))

            def gate_weights(g):
                dve.wait_ge(gate_exp, count(gate_exp, g, 1))
                link_gate(g, dve.scalar_tensor_tensor(out=sel[:, :, :], in0=sel[:, :, :], scalar=2.0,
                                                      in1=lex[:, :, :], op0=ALU.is_lt, op1=ALU.mult))
                link_gate(g, dve.tensor_reduce(lsm[:, :], sel[:, :, :], AX.X, ALU.add))
                link_gate(g, dve.reciprocal(lri[:, :], lsm[:, :]))
                assert gate_steps[0] == GATE_STEPS
                if any_yet(dn_out, g, 0):
                    dve.wait_ge(dn_out, count(dn_out, g, 0))
                dve.tensor_tensor(out=comb[:, :, :], in0=sel[:, :, :],
                                  in1=lri[:, :].unsqueeze(2).to_broadcast([P, T, NEXP]),
                                  op=ALU.mult).then_inc(comb_ready, 1)

            drive(dve, attention, feed_forward)

        @block.tensor
        def _(pe):
            pe.wait_ge(const_ready, 1)
            pe.wait_ge(small_in, 16 * n_small)
            for i in folds:
                kind, w, src, gain, job = pieces[i]
                s = stage[i % STAGES]
                pe.wait_ge(stage_in[i % STAGES], count_in(i))
                half = 0 if kind == "head" else 1
                K = P if half == 0 else EB
                bias = (b1c if gain is g1c else b2c)[0:K, half:half + 1]
                if job == "qkv":
                    for c in range(QK_PARTS):
                        pe.matmul(U[half][:, 24 + c:25 + c], s[0:K, c * P:(c + 1) * P], bias, start=True, stop=True)
                    mm = pe.matmul(U[half][:, 64:64 + E], bias.to_broadcast([K, P]), s[0:K, 2 * E:3 * E],
                                   start=True, stop=True)
                elif job == "gate":
                    mm = pe.matmul(U[half][:, 32:32 + NEXP], bias.to_broadcast([K, P]), s[0:K, 0:NEXP],
                                   start=True, stop=True)
                else:
                    for m in range(MH):
                        mm = pe.matmul(U[half][:, job * MH + m:job * MH + m + 1], s[0:K, m * P:(m + 1) * P], bias,
                                       start=True, stop=True)
                mm.then_inc(folded, 1)
            pe.wait_ge(ready, 1)

            def weights_first(dst, w, c0, m, x):
                cols = slice(c0, c0 + m)
                pe.matmul(dst, w.hi[:, cols], x[0][:, :], start=True, stop=False)
                pe.matmul(dst, w.hi[:, cols], x[1][:, :], start=False, stop=False)
                pe.matmul(dst, w.lo[:, cols], x[0][:, :], start=False, stop=False)
                pe.matmul(dst, w.tail[:, cols], x[2][:, :], start=False, stop=False)
                return pe.matmul(dst, w.tail[:, cols], x[3][:, :], start=False, stop=True)

            def tokens_first(dst, x, t, w, c0, m):
                cols, tok = slice(c0, c0 + m), slice(t * P, (t + 1) * P)
                pe.matmul(dst, x[0][:, tok], w.hi[:, cols], start=True, stop=False)
                pe.matmul(dst, x[0][:, tok], w.lo[:, cols], start=False, stop=False)
                pe.matmul(dst, x[1][:, tok], w.hi[:, cols], start=False, stop=False)
                pe.matmul(dst, x[2][:, tok], w.tail[:, cols], start=False, stop=False)
                return pe.matmul(dst, x[3][:, tok], w.tail[:, cols], start=False, stop=True)

            def to_columns(dst, src, c0):
                for t in range(T):
                    mm = pe.transpose(dst[:, t * P:(t + 1) * P], src[:, t, c0:c0 + P], ident[:, :])
                return mm

            def attention(g):
                for L in range(2):
                    for _ in range(3):
                        yield
                    pe.wait_ge(nx_ready, count(nx_ready, g, L + 1))
                    if any_yet(att_lo, g, 4 * L - 1):
                        pe.wait_ge(att_lo, count(att_lo, g, 4 * L - 1))
                    to_columns(A[0], nx, 0).then_inc(att_tr, 1)
                    if any_yet(att_lo, g, 4 * L):
                        pe.wait_ge(att_lo, count(att_lo, g, 4 * L))
                    to_columns(A[1], nx, P).then_inc(att_tr, 1)
                    yield
                    pe.wait_ge(att_lo, count(att_lo, g, 4 * L + 2))
                    if any_yet(res_done, g, 4 * L):
                        pe.wait_ge(res_done, count(res_done, g, 4 * L))
                    for c, bk in enumerate((2, 3, 0)):
                        weights_first(A[bk][:, :], wqkv[L], c * P, P, xa).then_inc(qk_done, 1)
                    yield
                    for t in range(T):
                        if t < 2:
                            pe.wait_ge(qk_out, count(qk_out, g, 4 * L + t + 1))
                        else:
                            pe.wait_ge(v_out, count(v_out, g, 4 * L + t - 1))
                        tokens_first(A[2 + t % 2][:, 0:E], xa, t, wqkv[L], 2 * E, E).then_inc(v_done, 1)
                        yield
                    for s in range(UPL + LAG):
                        if 2 <= s < UPL + 2:
                            u = s - 2
                            n = UPL * L + u
                            pe.wait_ge(exp_done, count(exp_done, g, n + 1))
                            if u < 2:
                                pe.wait_ge(v_out, count(v_out, g, 4 * L + u + 3))
                            else:
                                pe.wait_ge(pt_out, count(pt_out, g, n - 1))
                            for j in range(QH):
                                mm = pe.transpose(A[2 + u % 2][:, j * P:(j + 1) * P], prob[:, u % 2, j, :],
                                                  ident[:, :])
                            mm.then_inc(pt_done, 1)
                        if s < UPL:
                            n = UPL * L + s
                            t, c = divmod(s, 3)
                            rows = slice(EB * (c % 2), EB * (c % 2) + EB)
                            pe.wait_ge(qk_out, count(qk_out, g, 4 * L + 4))
                            pe.wait_ge(km_ready, count(km_ready, g, 2 * T * L + 2 * t + (2 if c == 2 else 1)))
                            if s >= 2:
                                pe.wait_ge(less_max, count(less_max, g, n - 1))
                            pe.matmul(A[s % 2][:, :], qk[rows, c // 2, t * P:(t + 1) * P],
                                      km2[:, :, :] if c == 2 else km[rows, t % 2, :, :],
                                      start=True, stop=True).then_inc(s_done, 1)
                        if s >= 3:
                            u = s - 3
                            n = UPL * L + u
                            t, c = divmod(u, 3)
                            pe.wait_ge(pt_out, count(pt_out, g, n + 1))
                            pe.wait_ge(v_out, count(v_out, g, 4 * L + t + 1))
                            if any_yet(ctx_done, g, n):
                                pe.wait_ge(ctx_done, count(ctx_done, g, n))
                            for j in range(QH):
                                mm = pe.matmul(OB[:, VW * j:VW * (j + 1)], probt[:, u % 2, j, :],
                                               val[:, t, QH * c + j, :], start=True, stop=True)
                            mm.then_inc(pv_done, 1)
                        yield
                    pe.wait_ge(ctx_done, count(ctx_done, g, UPL * (L + 1)))
                    pe.wait_ge(less_max, count(less_max, g, UPL * (L + 1)))
                    to_columns(A[0], nx, 0).then_inc(att_tr, 1)
                    to_columns(A[1], nx, P).then_inc(att_tr, 1)
                    yield
                    pe.wait_ge(att_lo, count(att_lo, g, 4 * L + 4))
                    for t in range(T):
                        if t >= 2:
                            pe.wait_ge(res_done, count(res_done, g, 4 * L + t - 1))
                        tokens_first(A[2 + t % 2][:, 0:E], xa, t, wout[L], 0, E).then_inc(op_done, 1)
                        if t % 2:
                            yield
                pe.wait_ge(res_done, count(res_done, g, 8))
                if any_yet(gelu_done, g, 0):
                    pe.wait_ge(gelu_done, count(gelu_done, g, 0))
                to_columns(U[0], r0, 0).then_inc(f_tr, 1)
                to_columns(U[1], r0, P).then_inc(f_tr, 1)
                yield

            def feed_forward(g):
                if not any_yet(dn_done, g, 0):
                    pe.wait_ge(w2_in, 16 * NB)
                for b in range(NB):
                    for m in range(MH):
                        u = MH * b + m
                        pe.wait_ge(f_lo, count(f_lo, g, 2 if b == 0 else 4))
                        if any_yet(gelu_done, g, u - 1):
                            pe.wait_ge(gelu_done, count(gelu_done, g, u - 1))
                        weights_first(U[u % 2][:, :], w1[b], m * P, P, fa).then_inc(up_done, 1)
                        yield
                        if b == 1 and m < GATE_PARTS:
                            if m == 0:
                                pe.wait_ge(f_lo, count(f_lo, g, 4))
                                pe.wait_ge(dn_out, count(dn_out, g, T))
                                for t in range(T):
                                    mm = tokens_first(DB[:, t * NEXP:(t + 1) * NEXP], fa, t, wgate, 0, NEXP)
                                mm.then_inc(gate_done, 1)
                            yield
                    for t in range(T):
                        d = T * b + t
                        if d == T:
                            pe.wait_ge(lg_ready, count(lg_ready, g, 1))
                        elif any_yet(dn_out, g, d):
                            pe.wait_ge(dn_out, count(dn_out, g, d))
                        dst, tok = DB[:, 0:E], slice(t * P, (t + 1) * P)
                        if b > 0:
                            pe.matmul(dst, ones[:, :], eb2[:, b - 1, :], start=True, stop=False)
                        for m in range(MH):
                            if t == 0:
                                pe.wait_ge(gelu_done, count(gelu_done, g, MH * b + m + 1))
                            mm = pe.matmul(dst, hid[:, b % 2, m, tok], w2[b][:, m, :], start=(b == 0 and m == 0),
                                           stop=(m == MH - 1))
                        mm.then_inc(dn_done, 1)
                        yield
                    if b == 0:
                        yield
                        yield
                        pe.wait_ge(n3_ready, count(n3_ready, g, 1))
                        pe.wait_ge(gelu_done, count(gelu_done, g, MH))
                        to_columns(U[0], n3, 0).then_inc(f_tr, 1)
                        to_columns(U[1], n3, P).then_inc(f_tr, 1)
                        yield

            drive(pe, attention, feed_forward)


def kernel(**inputs):
    import numpy as np
    import concourse.bacc as bacc
    from concourse.bass_utils import run_bass_kernel_spmd as run

    nc = bacc.Bacc("TRN2", target_bir_lowering=False, num_devices=1)
    arrays = {}

    def dram(name, a):
        a = np.ascontiguousarray(a)
        arrays[f"in_{name}"] = a
        return nc.dram_tensor(f"in_{name}", a.shape, mybir.dt.from_np(a.dtype), kind="ExternalInput").ap()

    i = {k: np.asarray(v) for k, v in inputs.items()}
    seqs, toks = i["x"].shape
    cols = np.concatenate([np.arange(a, b) for a, b in
                           ((0, P), (E, E + P), (P, E), (E + P, 2 * E), (2 * E, 3 * E))])
    args = [
        dram("ids", i["x"].T), dram("table", i["L0_tok_W"].T),
        [dram("qkv_w0", i["L0_attn_w_qkv"][:, cols]), dram("qkv_w1", i["L0_ffn_in_w"].T[:, cols])],
        [dram("qkv_b0", i["L0_attn_b_qkv"][cols]), dram("qkv_b1", i["L0_ffn_in_b"][cols])],
        [dram("out_w0", i["L0_attn_w_out"]), dram("out_w1", i["L0_ffn_out_w"].T)],
        [dram("out_b0", i["L0_attn_b_out"]), dram("out_b1", i["L0_ffn_out_b"])],
        dram("ln1_g", i["L0_ffn_ln1_g"]), dram("ln1_b", i["L0_ffn_ln1_b"]),
        dram("mlp_w1", i["L0_ffn_mlp_w1"]), dram("mlp_b1", i["L0_ffn_mlp_b1"].reshape(MH, P).T),
        dram("mlp_w2", i["L0_ffn_mlp_w2"]), dram("mlp_b2", i["L0_ffn_mlp_b2"]),
        dram("ln2_g", i["L0_ffn_ln2_g"]), dram("ln2_b", i["L0_ffn_ln2_b"]),
        dram("gate_w", i["L0_ffn_gate_w"].T), dram("gate_b", i["L0_ffn_gate_b"]),
        dram("exp_w1", i["L0_ffn_exp_w1"]),
        dram("exp_b1", i["L0_ffn_exp_b1"].reshape(NEXP * MH, P).T),
        dram("exp_w2", i["L0_ffn_exp_w2"]), dram("exp_b2", i["L0_ffn_exp_b2"]),
    ]
    out = nc.dram_tensor("out", (seqs, toks, E), F32, kind="ExternalOutput").ap()
    tower(nc, *args, out)
    r = run(nc, [arrays], core_ids=[0])
    return r.results[0]["out"]
```
